# Optimizing a Trainium2 kernel written in Bass

```python
import numpy as np
import jax
import jax.numpy as jnp

def _softmax(x, axis=-1):
    return jax.nn.softmax(x, axis=axis)

def _gelu(x):
    return jax.nn.gelu(x, approximate=True)

def _silu(x):
    return jax.nn.silu(x)

def _sigmoid(x):
    return jax.nn.sigmoid(x)

def _layernorm(x, axis=-1, eps=1e-05):
    m = jnp.mean(x, axis=axis, keepdims=True)
    v = jnp.var(x, axis=axis, keepdims=True)
    return (x - m) / jnp.sqrt(v + eps)

def _scatter_add(tgt, idx, src, axis=0):
    return tgt.at[idx].add(src)

def _segment_sum(src, seg, n):
    return jax.ops.segment_sum(src, seg, n)
kernel_name = 'mk_prb_d2_jaxref_r8_1374e3'

def setup_inputs(seed: int=0):
    np.random.seed(seed)
    _w = jnp.asarray

    def _L0_attn_setup():
        import jax, jax.numpy as jnp
        import numpy as np
        DIM = 128
        HEADS = 16
        HEAD_DIM = DIM // HEADS
        ROPE_BASE = 500000.0
        SCALE = HEAD_DIM ** (-0.5)

        def _rope_cos_sin(T, dtype=jnp.float32):
            inv_freq = 1.0 / ROPE_BASE ** (jnp.arange(0, HEAD_DIM, 2, dtype=jnp.float32) / HEAD_DIM)
            t = jnp.arange(T, dtype=jnp.float32)
            freqs = t[:, None] * inv_freq[None, :]
            emb = jnp.concatenate([freqs, freqs], axis=-1)
            return (jnp.cos(emb).astype(dtype), jnp.sin(emb).astype(dtype))

        def _rotate_half(x):
            x1, x2 = jnp.split(x, 2, axis=-1)
            return jnp.concatenate([-x2, x1], axis=-1)

        def _apply_rope(x, cos, sin):
            return x * cos + _rotate_half(x) * sin
        key = jax.random.key(seed)
        k1, k2, k3 = jax.random.split(key, 3)
        B, T = (4, 512)
        x = jax.random.normal(k1, (B, T, DIM), dtype=jnp.float32)
        W_qkv = jax.random.normal(k2, (DIM, 3 * DIM), dtype=jnp.float32) * DIM ** (-0.5)
        W_out = jax.random.normal(k3, (DIM, DIM), dtype=jnp.float32) * DIM ** (-0.5)
        return {'x': x, 'W_qkv': W_qkv, 'W_out': W_out}
    _L0_attn_in = _L0_attn_setup()

    def _L0_ffn_setup():
        import jax, jax.numpy as jnp
        import numpy as np
        H = 128
        I = 64
        E = 64
        G = 8
        TOPK_GROUP = 4
        K = 8
        I_SH = 128
        SCALE = 2.5

        def _route(x, router_w, e_bias):
            T = x.shape[0]
            scores = jax.nn.sigmoid(x.astype(jnp.float32) @ router_w.T.astype(jnp.float32))
            sfc = jax.lax.stop_gradient(scores) + e_bias[None, :]
            group_scores = jax.lax.top_k(sfc.reshape(T, G, E // G), 2)[0].sum(-1)
            _, gidx = jax.lax.top_k(group_scores, TOPK_GROUP)
            gmask = jax.nn.one_hot(gidx, G, dtype=sfc.dtype).sum(1)
            smask = jnp.repeat(gmask, E // G, axis=1)
            masked = jnp.where(smask > 0, sfc, 0.0)
            _, topk_idx = jax.lax.top_k(masked, K)
            w = jnp.take_along_axis(scores, topk_idx, axis=1)
            w = w / (w.sum(-1, keepdims=True) + 1e-20)
            return (topk_idx, w * SCALE)
        key = jax.random.key(seed)
        ks = jax.random.split(key, 9)
        s = 0.02
        return {'hidden_states': jax.random.normal(ks[0], (2, 128, H), jnp.float32), 'router_w': jax.random.normal(ks[1], (E, H), jnp.float32) * s, 'e_bias': jnp.zeros((E,), jnp.float32), 'Wg': jax.random.normal(ks[2], (E, H, I), jnp.float32) * s, 'Wu': jax.random.normal(ks[3], (E, H, I), jnp.float32) * s, 'Wd': jax.random.normal(ks[4], (E, I, H), jnp.float32) * s, 'SWg': jax.random.normal(ks[5], (H, I_SH), jnp.float32) * s, 'SWu': jax.random.normal(ks[6], (H, I_SH), jnp.float32) * s, 'SWd': jax.random.normal(ks[7], (I_SH, H), jnp.float32) * s}
    _L0_ffn_in = _L0_ffn_setup()

    def _L1_attn_setup():
        import jax, jax.numpy as jnp
        import numpy as np
        WINDOW = 4
        TOPK = 8
        key = jax.random.key(seed)
        ks = jax.random.split(key, 14)
        B, N, D = (4, 256, 128)
        s = 0.02
        w = lambda k_, shp: jax.random.normal(k_, shp, jnp.float32) * s
        return {'mu': jax.random.normal(ks[0], (B, N, D), jnp.float32), 'Wq': w(ks[1], (D, D)), 'bq': jnp.zeros((D,), jnp.float32), 'Wk': w(ks[2], (D, D)), 'bk': jnp.zeros((D,), jnp.float32), 'Wv': w(ks[3], (D, D)), 'bv': jnp.zeros((D,), jnp.float32), 'Wm1': w(ks[4], (2 * D, D)), 'bm1': jnp.zeros((D,), jnp.float32), 'Wm2': w(ks[5], (D, D)), 'bm2': jnp.zeros((D,), jnp.float32), 'Wo': w(ks[6], (2 * D, D)), 'bo': jnp.zeros((D,), jnp.float32)}
    _L1_attn_in = _L1_attn_setup()

    def _L1_ffn_setup():
        import jax, jax.numpy as jnp
        import numpy as np
        DIM = 128
        N_EXPERTS = 8
        D_FF = 256
        TOP_K = 2
        key = jax.random.key(seed)
        ks = jax.random.split(key, 5)
        s = 0.02
        return {'x': jax.random.normal(ks[0], (2, 256, DIM), dtype=jnp.float32), 'gate_w': jax.random.normal(ks[1], (N_EXPERTS, DIM), dtype=jnp.float32) * s, 'w1': jax.random.normal(ks[2], (N_EXPERTS, D_FF, DIM), dtype=jnp.float32) * s, 'w2': jax.random.normal(ks[3], (N_EXPERTS, DIM, D_FF), dtype=jnp.float32) * s, 'w3': jax.random.normal(ks[4], (N_EXPERTS, D_FF, DIM), dtype=jnp.float32) * s}
    _L1_ffn_in = _L1_ffn_setup()
    _d = {'L0_attn_x': _L0_attn_in['x'], 'L0_attn_W_qkv': _L0_attn_in['W_qkv'], 'L0_attn_W_out': _L0_attn_in['W_out'], 'L0_ffn_router_w': _L0_ffn_in['router_w'], 'L0_ffn_e_bias': _L0_ffn_in['e_bias'], 'L0_ffn_Wg': _L0_ffn_in['Wg'], 'L0_ffn_Wu': _L0_ffn_in['Wu'], 'L0_ffn_Wd': _L0_ffn_in['Wd'], 'L0_ffn_SWg': _L0_ffn_in['SWg'], 'L0_ffn_SWu': _L0_ffn_in['SWu'], 'L0_ffn_SWd': _L0_ffn_in['SWd'], 'L1_attn_Wq': _L1_attn_in['Wq'], 'L1_attn_bq': _L1_attn_in['bq'], 'L1_attn_Wk': _L1_attn_in['Wk'], 'L1_attn_bk': _L1_attn_in['bk'], 'L1_attn_Wv': _L1_attn_in['Wv'], 'L1_attn_bv': _L1_attn_in['bv'], 'L1_attn_Wm1': _L1_attn_in['Wm1'], 'L1_attn_bm1': _L1_attn_in['bm1'], 'L1_attn_Wm2': _L1_attn_in['Wm2'], 'L1_attn_bm2': _L1_attn_in['bm2'], 'L1_attn_Wo': _L1_attn_in['Wo'], 'L1_attn_bo': _L1_attn_in['bo'], 'L1_ffn_gate_w': _L1_ffn_in['gate_w'], 'L1_ffn_w1': _L1_ffn_in['w1'], 'L1_ffn_w2': _L1_ffn_in['w2'], 'L1_ffn_w3': _L1_ffn_in['w3']}
    _x0 = _d['L0_attn_x']
    _d['L0_attn_x'] = jax.random.normal(jax.random.fold_in(jax.random.key(seed), 1), (32, 256, 128), dtype=_x0.dtype)
    del _x0
    return _d

def reference(L0_attn_x, L0_attn_W_qkv, L0_attn_W_out, L0_ffn_router_w, L0_ffn_e_bias, L0_ffn_Wg, L0_ffn_Wu, L0_ffn_Wd, L0_ffn_SWg, L0_ffn_SWu, L0_ffn_SWd, L1_attn_Wq, L1_attn_bq, L1_attn_Wk, L1_attn_bk, L1_attn_Wv, L1_attn_bv, L1_attn_Wm1, L1_attn_bm1, L1_attn_Wm2, L1_attn_bm2, L1_attn_Wo, L1_attn_bo, L1_ffn_gate_w, L1_ffn_w1, L1_ffn_w2, L1_ffn_w3):

    def _L0_attn_ref(x, W_qkv, W_out):
        import jax, jax.numpy as jnp
        import numpy as np
        DIM = 128
        HEADS = 16
        HEAD_DIM = DIM // HEADS
        ROPE_BASE = 500000.0
        SCALE = HEAD_DIM ** (-0.5)

        def _rope_cos_sin(T, dtype=jnp.float32):
            inv_freq = 1.0 / ROPE_BASE ** (jnp.arange(0, HEAD_DIM, 2, dtype=jnp.float32) / HEAD_DIM)
            t = jnp.arange(T, dtype=jnp.float32)
            freqs = t[:, None] * inv_freq[None, :]
            emb = jnp.concatenate([freqs, freqs], axis=-1)
            return (jnp.cos(emb).astype(dtype), jnp.sin(emb).astype(dtype))

        def _rotate_half(x):
            x1, x2 = jnp.split(x, 2, axis=-1)
            return jnp.concatenate([-x2, x1], axis=-1)

        def _apply_rope(x, cos, sin):
            return x * cos + _rotate_half(x) * sin
        B, T, D = x.shape
        H, hd = (HEADS, HEAD_DIM)
        qkv = (x @ W_qkv).reshape(B, T, 3, H, hd).transpose(2, 0, 3, 1, 4)
        q, k, v = (qkv[0], qkv[1], qkv[2])
        cos, sin = _rope_cos_sin(T, q.dtype)
        q = _apply_rope(q, cos, sin)
        k = _apply_rope(k, cos, sin)
        q_feat = jax.nn.elu(q * SCALE) + 1.0
        k_feat = jax.nn.elu(k) + 1.0
        kv = jnp.einsum('bhtd,bhtv->bhdv', k_feat, v)
        k_sum = k_feat.sum(axis=2)
        denom = jnp.maximum(jnp.einsum('bhtd,bhd->bht', q_feat, k_sum), 1e-06)
        out = jnp.einsum('bhtd,bhdv->bhtv', q_feat, kv) / denom[..., None]
        out = out.transpose(0, 2, 1, 3).reshape(B, T, D)
        return out @ W_out

    def _L0_ffn_ref(hidden_states, router_w, e_bias, Wg, Wu, Wd, SWg, SWu, SWd):
        import jax, jax.numpy as jnp
        import numpy as np
        H = 128
        I = 64
        E = 64
        G = 8
        TOPK_GROUP = 4
        K = 8
        I_SH = 128
        SCALE = 2.5

        def _route(x, router_w, e_bias):
            T = x.shape[0]
            scores = jax.nn.sigmoid(x.astype(jnp.float32) @ router_w.T.astype(jnp.float32))
            sfc = jax.lax.stop_gradient(scores) + e_bias[None, :]
            group_scores = jax.lax.top_k(sfc.reshape(T, G, E // G), 2)[0].sum(-1)
            _, gidx = jax.lax.top_k(group_scores, TOPK_GROUP)
            gmask = jax.nn.one_hot(gidx, G, dtype=sfc.dtype).sum(1)
            smask = jnp.repeat(gmask, E // G, axis=1)
            masked = jnp.where(smask > 0, sfc, 0.0)
            _, topk_idx = jax.lax.top_k(masked, K)
            w = jnp.take_along_axis(scores, topk_idx, axis=1)
            w = w / (w.sum(-1, keepdims=True) + 1e-20)
            return (topk_idx, w * SCALE)
        orig_shape = hidden_states.shape
        x = hidden_states.reshape(-1, orig_shape[-1])
        T = x.shape[0]
        topk_idx, topk_w = _route(x, router_w, e_bias)
        coef = jnp.zeros((T, E), topk_w.dtype).at[jnp.arange(T)[:, None], topk_idx].add(topk_w)
        g = jnp.einsum('th,ehi->tei', x, Wg)
        u = jnp.einsum('th,ehi->tei', x, Wu)
        h = jax.nn.silu(g) * u * coef[:, :, None]
        moe_out = jnp.einsum('tei,eih->th', h, Wd)
        shared = jax.nn.silu(x @ SWg) * (x @ SWu) @ SWd
        return (moe_out + shared).reshape(orig_shape)

    def _L1_attn_ref(mu, Wq, bq, Wk, bk, Wv, bv, Wm1, bm1, Wm2, bm2, Wo, bo):
        import jax, jax.numpy as jnp
        import numpy as np
        WINDOW = 4
        TOPK = 8
        B, N, D = mu.shape
        padded = jnp.pad(mu, ((0, 0), (WINDOW, 0), (0, 0)))
        neighbors = jnp.stack([padded[:, WINDOW - w:WINDOW - w + N, :] for w in range(1, WINDOW + 1)], axis=2)
        self_exp = jnp.broadcast_to(mu[:, :, None, :], neighbors.shape)
        h = jnp.concatenate([self_exp, neighbors], axis=-1)
        h = jax.nn.silu(h @ Wm1 + bm1) @ Wm2 + bm2
        local_msgs = h.mean(axis=2)
        q = mu @ Wq + bq
        k = mu @ Wk + bk
        v = mu @ Wv + bv
        scores = jnp.einsum('bnd,bmd->bnm', q, k) / np.sqrt(D).astype(np.float32)
        causal_mask = jnp.triu(jnp.ones((N, N), dtype=bool), k=1)
        scores = jnp.where(causal_mask[None], -jnp.inf, scores)
        if N > TOPK:
            topk_v, topk_i = jax.lax.top_k(scores, TOPK)
            bi = jnp.arange(B)[:, None, None]
            ni = jnp.arange(N)[None, :, None]
            sparse = jnp.full_like(scores, -jnp.inf).at[bi, ni, topk_i].set(topk_v)
            attn = jax.nn.softmax(sparse, axis=-1)
        else:
            attn = jax.nn.softmax(scores, axis=-1)
        glob = jnp.einsum('bnm,bmd->bnd', attn, v)
        return jnp.concatenate([local_msgs, glob], axis=-1) @ Wo + bo

    def _L1_ffn_ref(x, gate_w, w1, w2, w3):
        import jax, jax.numpy as jnp
        import numpy as np
        DIM = 128
        N_EXPERTS = 8
        D_FF = 256
        TOP_K = 2
        orig_shape = x.shape
        xf = x.reshape(-1, orig_shape[-1])
        scores = jnp.einsum('td,ed->te', xf, gate_w)
        probs = jax.nn.softmax(scores.astype(jnp.float32), axis=-1)
        weights, idx = jax.lax.top_k(probs, TOP_K)
        weights = weights / jnp.sum(weights, axis=-1, keepdims=True)
        weights = weights.astype(x.dtype)
        x1 = jax.nn.silu(jnp.einsum('td,efd->tef', xf, w1))
        x3 = jnp.einsum('td,efd->tef', xf, w3)
        out_all = jnp.einsum('tef,edf->ted', x1 * x3, w2)
        expert_outs = jnp.take_along_axis(out_all, idx[:, :, None], axis=1)
        result = jnp.einsum('tkd,tk->td', expert_outs, weights)
        return result.reshape(orig_shape)
    x = L0_attn_x
    xn = _layernorm(x, axis=-1)
    x = x + _L0_attn_ref(xn, L0_attn_W_qkv, L0_attn_W_out) + _L0_ffn_ref(xn, L0_ffn_router_w, L0_ffn_e_bias, L0_ffn_Wg, L0_ffn_Wu, L0_ffn_Wd, L0_ffn_SWg, L0_ffn_SWu, L0_ffn_SWd)
    xn = _layernorm(x, axis=-1)
    x = x + _L1_attn_ref(xn, L1_attn_Wq, L1_attn_bq, L1_attn_Wk, L1_attn_bk, L1_attn_Wv, L1_attn_bv, L1_attn_Wm1, L1_attn_bm1, L1_attn_Wm2, L1_attn_bm2, L1_attn_Wo, L1_attn_bo) + _L1_ffn_ref(xn, L1_ffn_gate_w, L1_ffn_w1, L1_ffn_w2, L1_ffn_w3)
    return x

_drawn_inputs = setup_inputs


def setup_inputs(seed=0):
    import zlib

    import numpy as np

    out = dict(_drawn_inputs(seed))
    spreads = {'L0_ffn_e_bias': (0.0, 0.8),
     'L1_attn_bq': (0.0, 2.0),
     'L1_attn_bk': (0.0, 2.0),
     'L1_attn_bv': (0.0, 2.0),
     'L1_attn_bm1': (0.0, 2.0),
     'L1_attn_bm2': (0.0, 1.984),
     'L1_attn_bo': (0.0, 0.55)}
    factors = {'L0_ffn_router_w': 8.0,
     'L0_ffn_Wg': 8.0,
     'L0_ffn_Wu': 8.0,
     'L0_ffn_Wd': 8.0,
     'L0_ffn_SWg': 8.0,
     'L0_ffn_SWu': 8.0,
     'L0_ffn_SWd': 8.0,
     'L1_attn_Wq': 23.64,
     'L1_attn_Wk': 19.575,
     'L1_attn_Wv': 16.81,
     'L1_attn_Wm1': 8.0,
     'L1_attn_Wm2': 7.825,
     'L1_ffn_gate_w': 8.0,
     'L1_ffn_w1': 8.0,
     'L1_ffn_w2': 8.0,
     'L1_ffn_w3': 8.0}
    for name, (base, spread) in spreads.items():
        noise = np.random.default_rng([zlib.crc32(name.encode()), seed]).standard_normal(out[name].shape)
        drawn = base * np.exp(spread * noise) if base else spread * noise
        out[name] = jnp.asarray(drawn.astype(out[name].dtype))
    for name, factor in factors.items():
        out[name] = (out[name] * factor).astype(out[name].dtype)
    return out
```

```python
from contextlib import ExitStack

import concourse.bass as bass
import numpy as np
from concourse import mybir

FP32 = mybir.dt.float32
FP32R = mybir.dt.float32r
ALU = mybir.AluOpType
ACT = mybir.ActivationFunctionType
AX = mybir.AxisListType.X

P = 128
SEQ = 256
TOKENS = 32 * SEQ
CHUNK = 512
ROWS = CHUNK // P
SEQS = CHUNK // SEQ
CHUNKS = TOKENS // CHUNK
HEADS, HEAD = 16, 8
ROPE_BASE = 500000.0
EXPERTS0, FF0, GROUPS0, TOP_GROUPS0, TOP0, SCALE0 = 64, 64, 8, 4, 8, 2.5
EXPERTS1, FF1, TOP1 = 8, 256, 2
WINDOW, TOP_KEYS = 4, 8
TILES0 = EXPERTS0 * FF0 // P + 1
TILES1 = EXPERTS1 * FF1 // P
FAR = -1.0e30
EPS_LN, EPS_DEN, EPS_W = 1e-5, 1e-6, 1e-20
KEYS = [(0, P), (P, SEQ)]
KEYCOLS = P + SEQ
STAGES_W = 3
LAG = 3


class Stage:

    def __init__(self, sem):
        self.sem, self.n = sem, 0

    def done(self, by=1):
        self.n += by
        return (self, self.n)


class Line:

    def __init__(self):
        self.items, self.seen = [], {}

    def put(self, stage, waits, *instructions, by=1):
        need = []
        for mark in waits:
            if mark is not None and self.seen.get(mark[0], 0) < mark[1]:
                self.seen[mark[0]] = mark[1]
                need.append(mark)
        mark = stage.done(by)
        self.items.append((need, instructions, stage, by))
        return mark

    def chain(self, stage, waits, *instructions):
        mark = None
        for n, one in enumerate(instructions):
            mark = self.put(stage, waits if n == 0 else [mark], one)
        return mark

    def run(self, engine):
        for need, instructions, stage, by in self.items:
            for sem_stage, value in need:
                engine.wait_ge(sem_stage.sem, value)
            for one in instructions:
                last = one()
            last.then_inc(stage.sem, by)


def build_program(nc, x, ffn_w, att0_w, att0_f, att0_c, e_bias, att1_w, att1_f, att1_b, att1_c, common_c, out):
    ctx = ExitStack()
    with ctx:
        def sb(name, shape, dtype=FP32, within=ctx):
            return within.enter_context(nc.sbuf_tensor(name, [P] + list(shape), dtype))

        def stage(name):
            return Stage(ctx.enter_context(nc.semaphore(name)))

        xres = sb("xres", [CHUNKS, ROWS, P])
        w_gu = sb("w_gu", [TILES0, 2, 2, P], FP32R)
        w_dn = sb("w_dn", [TILES0, 2, P], FP32R)
        w_raw = sb("w_raw", [STAGES_W, 3, P])
        xnT = sb("xnT", [2, 2, CHUNK], FP32R)
        coefT = sb("coefT", [2, CHUNK], FP32R)
        coef = sb("coef", [ROWS, 2, 64])
        silu_h = sb("silu_h", [3, CHUNK])
        h_hi = sb("h_hi", [3, CHUNK], FP32R)
        h_lo = sb("h_lo", [3, CHUNK], FP32R)
        swing = sb("swing", [CHUNK])
        mix_a = sb("mix_a", [CHUNK])
        mix_b = sb("mix_b", [CHUNK])
        common = sb("common", [P + 64 + 64])
        ident, pick, earlier = common[:, 0:P], common[:, P:P + 64], common[:, P + 64:P + 128]
        pick_pair = sb("pick_pair", [2, 2, 64], FP32R)
        stats = sb("stats", [ROWS, 6])
        mean_var = sb("mean_var", [ROWS, 2])
        rstd = sb("rstd", [ROWS])
        minus_half = sb("minus_half", [ROWS])

        in0 = ExitStack()
        c0 = sb("att0_const", [P + 4 * SEQ], within=in0)
        same_head = c0[:, 0:P]
        cosq, sinq, cosk, sink = (c0[:, P + n * SEQ:P + (n + 1) * SEQ] for n in range(4))
        w0 = sb("w0", [2, 5 * P + EXPERTS0], FP32R, within=in0)
        w_out = sb("w_out", [P], within=in0)
        bias0 = sb("bias0", [EXPERTS0], within=in0)
        ones = sb("ones", [P], within=in0)
        kf = sb("kf", [CHUNK], within=in0)
        qf = sb("qf", [CHUNK], within=in0)
        tmp0 = sb("tmp0", [CHUNK], within=in0)
        v0 = sb("v0", [CHUNK], within=in0)
        kv = sb("kv", [SEQS, 2, P], within=in0)
        score0 = sb("score0", [ROWS * EXPERTS0], within=in0)
        sfc = sb("sfc", [ROWS * EXPERTS0], within=in0)
        ra = sb("ra", [ROWS * 64], within=in0)
        rb = sb("rb", [ROWS * 64], within=in0)
        hi4 = sb("hi4", [ROWS * GROUPS0, 4], within=in0)
        lo4 = sb("lo4", [ROWS * GROUPS0, 4], within=in0)
        hi2 = sb("hi2", [ROWS * GROUPS0, 2], within=in0)
        mi2 = sb("mi2", [ROWS * GROUPS0, 2], within=in0)
        lo2 = sb("lo2", [ROWS * GROUPS0, 2], within=in0)
        g_a = sb("g_a", [ROWS * GROUPS0], within=in0)
        g_b = sb("g_b", [ROWS * GROUPS0], within=in0)
        best0 = sb("best0", [ROWS, 8], within=in0)
        wsum0 = sb("wsum0", [ROWS], within=in0)
        in0.close()

        in1 = ExitStack()
        causal = sb("causal", [KEYCOLS], within=in1)
        w1 = sb("w1", [2, 5 * P + EXPERTS1], FP32R, within=in1)
        f1 = sb("f1", [3 * P], within=in1)
        w_m2, w_ol, w_og = (f1[:, n * P:(n + 1) * P] for n in range(3))
        b1 = sb("b1", [6], within=in1)
        b_q, b_k, b_v, b_m1, b_m2, b_o = (b1[:, n:n + 1] for n in range(6))
        qT = sb("qT", [CHUNK], within=in1)
        kT = sb("kT", [CHUNK], within=in1)
        v1 = sb("v1", [CHUNK], within=in1)
        scores = sb("scores", [SEQS, KEYCOLS], within=in1)
        rest = sb("rest", [SEQS, KEYCOLS], within=in1)
        near = sb("near", [SEQS, WINDOW + SEQ], within=in1)
        msg = sb("msg", [3, CHUNK], within=in1)
        best1 = sb("best1", [ROWS, 8], within=in1)
        top_neg = sb("top_neg", [ROWS], within=in1)
        psum1 = sb("psum1", [ROWS], within=in1)
        gate = sb("gate", [ROWS, EXPERTS1], within=in1)
        gsel = sb("gsel", [ROWS, EXPERTS1], within=in1)
        ga = sb("ga", [ROWS * 64], within=in1)
        gb = sb("gb", [ROWS * 64], within=in1)
        gsum = sb("gsum", [ROWS], within=in1)
        in1.close()

        def bank(name):
            return ctx.enter_context(nc.psum_tensor(name, [P, CHUNK], FP32))

        ps_gate = [bank("ps_gate0"), bank("ps_gate1")]
        ps_up = [bank("ps_up0"), bank("ps_up1")]
        ps_coef = bank("ps_coef")
        ps_y = bank("ps_y")
        ps_side = [bank("ps_side0"), bank("ps_side1")]

        x_in = [stage(f"x_in{c}") for c in range(CHUNKS)]
        w_in = [stage(f"w_in{n}") for n in range(STAGES_W)]
        const_in = stage("const_in")
        att0_in = stage("att0_in")
        att1_in = stage("att1_in")
        att1_raw_in = stage("att1_raw_in")
        stored = stage("stored")
        pe_gate, pe_up, pe_coef, pe_down = (stage(n) for n in ("pe_gate", "pe_up", "pe_coef", "pe_down"))
        act_silu, act_hi, act_whi, act_y = (stage(n) for n in ("act_silu", "act_hi", "act_whi", "act_y"))
        dve_up, dve_coef, dve_wlo = (stage(n) for n in ("dve_up", "dve_coef", "dve_wlo"))
        pool_lo, pool_pick = stage("pool_lo"), stage("pool_pick")
        pe_side, act_side, dve_side, pool_side = (stage(n) for n in ("pe_side", "act_side", "dve_side", "pool_side"))
        dve_setup, pool_setup, act_setup = stage("dve_setup"), stage("pool_setup"), stage("act_setup")

        PE, SCAL, DVE, POOL, SP = (Line() for _ in range(5))
        T, A, V, G = nc.tensor, nc.scalar, nc.vector, nc.gpsimd

        def f32(ap):
            return ap.bitcast(FP32)

        def mm3(dst, w, m, start=True, stop=True):
            return [lambda: T.matmul(dst, w[0], m[0], start=start, stop=False),
                    lambda: T.matmul(dst, w[1], m[0], start=False, stop=False),
                    lambda: T.matmul(dst, w[0], m[1], start=False, stop=stop)]

        def mm(dst, w, m, start=True, stop=True):
            return [lambda: T.matmul(dst, w, m, start=start, stop=stop)]

        def load(stg, dst, src):
            return SP.put(stg, [], lambda: nc.sync.dma_start(dst, src), by=16)

        x_rows = x.rearrange("(c r p) d -> c p r d", r=ROWS, p=P)
        out_rows = out.rearrange("(c r p) d -> c p r d", r=ROWS, p=P)
        raw0 = silu_h[:, :, :].rearrange("p a b -> p (a b)")[:, 0:5 * P + EXPERTS0]
        x_ready = [None] * CHUNKS
        x_ready[0] = load(x_in[0], xres[:, 0], x_rows[0])
        common_ready = load(const_in, common[:, :], common_c)
        load(att0_in, raw0, att0_w)
        load(att0_in, c0[:, :], att0_c)
        load(att0_in, w_out[:, :], att0_f)
        att0_ready = load(att0_in, bias0[:, :], e_bias.partition_broadcast(P))

        w_split = [None] * (TILES0 + TILES1)
        w_loaded = [None] * (TILES0 + TILES1)

        def load_tile(n):
            waits = list(w_split[n - STAGES_W]) if n >= STAGES_W else []
            w_loaded[n] = SP.put(w_in[n % STAGES_W], waits,
                                 lambda: nc.sync.dma_start(w_raw[:, n % STAGES_W], ffn_w[n].rearrange("p (k d) -> p k d", k=3)), by=16)

        for n in range(STAGES_W):
            load_tile(n)
        for c in range(1, min(3, CHUNKS)):
            x_ready[c] = load(x_in[c], xres[:, c], x_rows[c])

        def tile_weights(j):
            gu, dn = w_gu[:, j], w_dn[:, j]
            return (gu[:, 0, 0], gu[:, 0, 1]), (gu[:, 1, 0], gu[:, 1, 1]), (dn[:, 0], dn[:, 1])

        def split_tile(layer, j, free=()):
            n = j + layer * TILES0
            raw = w_raw[:, n % STAGES_W]
            gu, dn = w_gu[:, j], w_dn[:, j]
            hi = SCAL.put(act_whi, [w_loaded[n], *free],
                          lambda: A.copy(gu[:, :, 0], raw[:, 0:2]),
                          lambda: A.copy(dn[:, 0], raw[:, 2]))
            lo = DVE.put(dve_wlo, [hi],
                         lambda: V.tensor_tensor(gu[:, :, 1], raw[:, 0:2], f32(gu[:, :, 0]), ALU.subtract),
                         lambda: V.tensor_tensor(dn[:, 1], raw[:, 2], f32(dn[:, 0]), ALU.subtract))
            w_split[n] = (hi, lo)
            if n + STAGES_W < TILES0 + TILES1:
                load_tile(n + STAGES_W)

        pow_ready = DVE.put(dve_setup, [], lambda: V.memset(minus_half[:, :], -0.5))
        ones_ready = DVE.put(dve_setup, [], lambda: V.memset(ones[:, :], 1.0))

        def split_small(dst, raw, waits):
            hi = SCAL.put(act_setup, waits, lambda: A.copy(dst[:, 0], raw))
            return DVE.put(dve_setup, [hi], lambda: V.tensor_tensor(dst[:, 1], raw, f32(dst[:, 0]), ALU.subtract))

        w0_ready = split_small(w0, raw0, [att0_ready])

        side_free = [w0_ready, w0_ready]
        side_turn = [0]

        def side_bank():
            side_turn[0] ^= 1
            return side_turn[0], ps_side[side_turn[0]]

        xnT_free = [None, None]
        coefT_free = [None, None]
        swing_free = [None]
        xnT_ready, coefT_ready, mix_ready = {}, {}, {}
        mix_free = [None]
        coef_free = [None]

        def layer_norm(key, c, x_mark):
            buf = key % 2
            mark = DVE.put(dve_side, [x_mark],
                           *[lambda r=r: V.bn_stats(stats[:, r], xres[:, c, r]) for r in range(ROWS)])
            mark = DVE.put(dve_side, [mark],
                           *[lambda r=r: V.bn_aggr(mean_var[:, r], stats[:, r]) for r in range(ROWS)])
            mark = DVE.put(dve_side, [mark], lambda: V.tensor_scalar(rstd[:, :], mean_var[:, :, 1], EPS_LN, None, ALU.add))
            yield
            mark = POOL.put(pool_side, [mark, pow_ready],
                            lambda: G.tensor_tensor(rstd[:, :], rstd[:, :], minus_half[:, :], ALU.pow))
            yield
            mark = DVE.put(dve_side, [mark, swing_free[0]],
                           *[lambda r=r: V.tensor_scalar(swing[:, r * P:(r + 1) * P], xres[:, c, r], mean_var[:, r, 0:1],
                                                         rstd[:, r:r + 1], ALU.subtract, ALU.mult) for r in range(ROWS)])
            yield
            b, ps = side_bank()
            mark = PE.put(pe_side, [mark, side_free[b], common_ready],
                          *[lambda r=r: T.transpose(ps[:, r * P:(r + 1) * P], swing[:, r * P:(r + 1) * P], ident)
                            for r in range(ROWS)])
            swing_free[0] = mark
            yield
            hi = SCAL.put(act_side, [mark, xnT_free[buf]], lambda: A.copy(xnT[:, buf, 0], ps[:, :]))
            yield
            lo = DVE.put(dve_side, [hi], lambda: V.tensor_tensor(xnT[:, buf, 1], ps[:, :], f32(xnT[:, buf, 0]), ALU.subtract))
            side_free[b] = lo
            xnT_ready[key] = lo
            yield

        def rank_among_8(values, rows, above, equal, count, waits):
            shape = [P, rows, 8, 8]
            mine = values.unsqueeze(3).to_broadcast(shape)
            other = values.unsqueeze(2).to_broadcast(shape)
            first = earlier.rearrange("p (g h) -> p g h", g=8).unsqueeze(1).to_broadcast(shape)
            ab = above.rearrange("p (r g h) -> p r g h", g=8, h=8)
            eq = equal.rearrange("p (r g h) -> p r g h", g=8, h=8)
            m = DVE.put(dve_side, waits, lambda: V.tensor_tensor(ab, other, mine, ALU.is_gt),
                        lambda: V.tensor_tensor(eq, other, mine, ALU.is_equal))
            return DVE.chain(dve_side, [m],
                             lambda: V.tensor_tensor(eq, eq, first, ALU.mult),
                             lambda: V.tensor_tensor(above, above, equal, ALU.add),
                             lambda: V.tensor_reduce(count, ab, axis=AX, op=ALU.add))

        def coef_to_columns(key, mark):
            buf = key % 2
            b, ps = side_bank()
            flat = coef[:, :, :, :].rearrange("p r a e -> p r (a e)")
            mark = PE.put(pe_side, [mark, side_free[b]],
                          *[lambda r=r: T.transpose(ps[:, r * P:(r + 1) * P], flat[:, r], ident) for r in range(ROWS)])
            coef_free[0] = mark
            yield
            hi = SCAL.put(act_side, [mark, coefT_free[buf]], lambda: A.copy(coefT[:, buf], ps[:, :]))
            yield
            lo = DVE.put(dve_side, [hi], lambda: V.tensor_tensor(coefT[64:P, buf], ps[64:P, :], f32(coefT[64:P, buf]), ALU.subtract))
            side_free[b] = lo
            coefT_ready[key] = lo
            yield

        def side0(key, c):
            yield from layer_norm(key, c, x_ready[c])
            buf = key % 2
            xt = (xnT[:, buf, 0], xnT[:, buf, 1])
            ready = [xnT_ready[key], w0_ready]

            def w(lo, hi):
                return (w0[:, 0, lo:hi], w0[:, 1, lo:hi])

            def rows(r):
                return (xt[0][:, r * P:(r + 1) * P], xt[1][:, r * P:(r + 1) * P])

            b, ps_r = side_bank()
            logits = ps_r[:, 0:ROWS * EXPERTS0]
            mark = PE.put(pe_side, ready + [side_free[b]],
                          *[f for r in range(ROWS) for f in
                            mm3(ps_r[:, r * EXPERTS0:(r + 1) * EXPERTS0], rows(r), w(5 * P, 5 * P + EXPERTS0))])
            yield
            kept = DVE.put(dve_side, [mark], lambda: V.tensor_copy(score0[:, :], logits))
            side_free[b] = kept
            for r in range(ROWS):
                b, ps = side_bank()
                mark = PE.put(pe_side, [side_free[b]], *mm3(ps[:, 0:3 * P], rows(r), w(2 * P, 5 * P)))
                yield
                half = (r % 2) * P
                DVE.put(dve_side, [mark],
                        lambda ps=ps, r=r, half=half: V.tensor_tensor(kf[:, r * P:(r + 1) * P], ps[:, 0:P], cosk[:, half:half + P], ALU.mult))
                mark = DVE.put(dve_side, [mark],
                               lambda ps=ps, r=r, half=half: V.tensor_tensor(tmp0[:, r * P:(r + 1) * P], ps[:, P:2 * P], sink[:, half:half + P], ALU.mult))
                side_free[b] = SCAL.put(act_side, [mark], lambda ps=ps, r=r: A.copy(v0[:, r * P:(r + 1) * P], ps[:, 2 * P:3 * P]))
                v_ready = side_free[b]
            k_rope = POOL.put(pool_side, [mark], lambda: G.tensor_tensor(kf[:, :], kf[:, :], tmp0[:, :], ALU.add))
            b, ps = side_bank()
            mark = PE.put(pe_side, [side_free[b]], *mm3(ps[:, :], w(0, P), xt))
            by_seq = [P, SEQS, SEQ]

            def seqs(ap):
                return ap.rearrange("p (s t) -> p s t", s=SEQS)

            yield
            side_free[b] = DVE.put(dve_side, [mark], lambda ps=ps: V.tensor_tensor(
                seqs(qf[:, :]), seqs(ps[:, :]), cosq.unsqueeze(1).to_broadcast(by_seq), ALU.mult))
            b, ps = side_bank()
            mark = PE.put(pe_side, [side_free[b]], *mm3(ps[:, :], w(P, 2 * P), xt))
            yield
            mark = DVE.put(dve_side, [mark, k_rope], lambda ps=ps: V.tensor_tensor(
                seqs(tmp0[:, :]), seqs(ps[:, :]), sinq.unsqueeze(1).to_broadcast(by_seq), ALU.mult))
            side_free[b] = mark
            q_rope = POOL.put(pool_side, [mark], lambda: G.tensor_tensor(qf[:, :], qf[:, :], tmp0[:, :], ALU.add))
            yield
            k_min = DVE.put(dve_side, [k_rope, swing_free[0]], lambda: V.tensor_scalar(swing[:, :], kf[:, :], 0.0, None, ALU.min))
            yield
            q_min = DVE.put(dve_side, [q_rope], lambda: V.tensor_scalar(tmp0[:, :], qf[:, :], 0.0, None, ALU.min))
            yield
            k_exp = SCAL.put(act_side, [k_min], lambda: A.activation(swing[:, :], swing[:, :], ACT.Exp))
            q_exp = SCAL.put(act_side, [q_min], lambda: A.activation(tmp0[:, :], tmp0[:, :], ACT.Exp))
            r_exp = SCAL.put(act_side, [kept], lambda: A.activation(score0[:, :], score0[:, :], ACT.Exp, scale=-1.0))
            yield
            kf_ready = DVE.put(dve_side, [k_exp], lambda: V.scalar_tensor_tensor(kf[:, :], kf[:, :], 0.0, swing[:, :], ALU.max, ALU.add))
            swing_free[0] = kf_ready
            qf_ready = DVE.put(dve_side, [q_exp], lambda: V.scalar_tensor_tensor(qf[:, :], qf[:, :], 0.0, tmp0[:, :], ALU.max, ALU.add))
            yield
            b, ps = side_bank()
            products = []
            for s in range(SEQS):
                for n in range(2):
                    for r in (2 * s, 2 * s + 1):
                        rhs = v0[:, r * P:(r + 1) * P] if n == 0 else ones[:, :]
                        products += mm(ps[:, (2 * s + n) * P:(2 * s + n + 1) * P], kf[:, r * P:(r + 1) * P], rhs,
                                       start=r == 2 * s, stop=r == 2 * s + 1)
            mark = PE.put(pe_side, [kf_ready, v_ready, ones_ready, side_free[b]], *products)
            score = DVE.chain(dve_side, [r_exp],
                              lambda: V.tensor_scalar(score0[:, :], score0[:, :], 1.0, None, ALU.add),
                              lambda: V.reciprocal(score0[:, :], score0[:, :]))
            by_tok = [P, ROWS, EXPERTS0]
            row = lambda ap: ap.rearrange("p (r e) -> p r e", r=ROWS)
            choice = DVE.put(dve_side, [score], lambda: V.tensor_tensor(
                row(sfc[:, :]), row(score0[:, :]), bias0[:, :].unsqueeze(1).to_broadcast(by_tok), ALU.add))
            yield
            kv_ready = DVE.put(dve_side, [mark], lambda ps=ps: V.tensor_tensor(
                kv[:, :, :, :].rearrange("p s n d -> p (s n) d"), ps[:, :].rearrange("p (a d) -> p a d", d=P),
                same_head.unsqueeze(1).to_broadcast([P, 2 * SEQS, P]), ALU.mult))
            side_free[b] = kv_ready
            yield
            terms = []
            for n in range(2):
                b, ps = side_bank()
                terms.append((b, ps))
                mark = PE.put(pe_side, [kv_ready, qf_ready, side_free[b]],
                              *[f for s in range(SEQS) for f in
                                mm(ps[:, s * SEQ:(s + 1) * SEQ], kv[:, s, n], qf[:, s * SEQ:(s + 1) * SEQ])])
            yield
            mark2 = DVE.chain(dve_side, [mark],
                              lambda: V.tensor_scalar(tmp0[:, :], terms[1][1][:, :], EPS_DEN, None, ALU.max),
                              lambda: V.reciprocal(tmp0[:, :], tmp0[:, :]))
            yield
            mark = DVE.put(dve_side, [mark2, mix_free[0]], lambda: V.tensor_tensor(mix_a[:, :], terms[0][1][:, :], tmp0[:, :], ALU.mult))
            side_free[terms[0][0]] = side_free[terms[1][0]] = mark
            mix_ready[key] = mark
            yield
            grp = sfc[:, :].rearrange("p (g e) -> p g e", e=8)
            m = DVE.put(dve_side, [choice],
                        lambda: V.tensor_tensor(hi4[:, :, :], grp[:, :, 0:4], grp[:, :, 4:8], ALU.max),
                        lambda: V.tensor_tensor(lo4[:, :, :], grp[:, :, 0:4], grp[:, :, 4:8], ALU.min))
            yield
            m = DVE.put(dve_side, [m],
                        lambda: V.tensor_tensor(hi2[:, :, :], hi4[:, :, 0:2], hi4[:, :, 2:4], ALU.max),
                        lambda: V.tensor_tensor(mi2[:, :, :], hi4[:, :, 0:2], hi4[:, :, 2:4], ALU.min),
                        lambda: V.tensor_tensor(lo2[:, :, :], lo4[:, :, 0:2], lo4[:, :, 2:4], ALU.max))
            m = DVE.put(dve_side, [m], lambda: V.tensor_tensor(lo2[:, :, :], lo2[:, :, :], mi2[:, :, :], ALU.max))
            m = DVE.put(dve_side, [m],
                        lambda: V.tensor_tensor(mi2[:, :, 0], hi2[:, :, 0], hi2[:, :, 1], ALU.min),
                        lambda: V.tensor_tensor(g_a[:, :], hi2[:, :, 0], hi2[:, :, 1], ALU.max))
            yield
            m = DVE.chain(dve_side, [m],
                          lambda: V.tensor_tensor(lo2[:, :, 0], lo2[:, :, 0], lo2[:, :, 1], ALU.max),
                          lambda: V.tensor_tensor(lo2[:, :, 0], lo2[:, :, 0], mi2[:, :, 0], ALU.max),
                          lambda: V.tensor_tensor(g_a[:, :], g_a[:, :], lo2[:, :, 0], ALU.add))
            yield
            m = rank_among_8(g_a[:, :].rearrange("p (r g) -> p r g", r=ROWS), ROWS, ra[:, :], rb[:, :],
                             g_b[:, :].rearrange("p (r g) -> p r g", r=ROWS), [m, common_ready])
            yield
            m = DVE.put(dve_side, [m], lambda: V.tensor_scalar(g_b[:, :], g_b[:, :], TOP_GROUPS0 - 0.5, None, ALU.is_lt))
            m = DVE.chain(dve_side, [m],
                          lambda: V.tensor_tensor(grp, grp, g_b[:, :].unsqueeze(2).to_broadcast([P, ROWS * GROUPS0, 8]), ALU.mult),
                          lambda: V.tensor_scalar(sfc[:, :], sfc[:, :], 0.0, None, ALU.add))
            yield
            m = DVE.put(dve_side, [m], *[lambda r=r: V.max(best0[:, r], row(sfc[:, :])[:, r]) for r in range(ROWS)])
            yield
            m = DVE.put(dve_side, [m], *[lambda r=r: V.match_replace(
                out=row(ra[:, :])[:, r], in_to_replace=best0[:, r], in_values=row(sfc[:, :])[:, r], imm_value=FAR) for r in range(ROWS)])
            yield
            m = DVE.chain(dve_side, [m],
                          lambda: V.tensor_tensor(ra[:, :], ra[:, :], sfc[:, :], ALU.not_equal),
                          lambda: V.tensor_tensor(ra[:, :], ra[:, :], score0[:, :], ALU.mult),
                          lambda: V.tensor_reduce(wsum0[:, :], row(ra[:, :]), axis=AX, op=ALU.add))
            yield
            m = DVE.chain(dve_side, [m],
                          lambda: V.tensor_scalar(wsum0[:, :], wsum0[:, :], EPS_W, None, ALU.add),
                          lambda: V.reciprocal(wsum0[:, :], wsum0[:, :]),
                          lambda: V.tensor_tensor(row(ra[:, :]), row(ra[:, :]), wsum0[:, :].unsqueeze(2).to_broadcast(by_tok), ALU.mult))
            m = DVE.put(dve_side, [m, coef_free[0]],
                        *[lambda n=n: V.tensor_scalar(coef[:, :, n], row(ra[:, :]), SCALE0, None, ALU.mult) for n in range(2)])
            yield
            yield from coef_to_columns(key, m)

        att1 = {}

        def side1_setup():
            over = [side_free[0], side_free[1], coefT_ready[CHUNKS - 1], mix_ready[CHUNKS - 1]]
            raw1 = scores[:, :, :].rearrange("p a b -> p (a b)")[:, 0:5 * P + EXPERTS1]
            SP.put(att1_raw_in, over, lambda: nc.sync.dma_start(raw1, att1_w), by=16)
            raw_ready = (att1_raw_in, att1_raw_in.n)
            load(att1_in, causal[:, :], att1_c)
            load(att1_in, f1[:, :], att1_f)
            att1["in"] = load(att1_in, b1[:, :], att1_b)
            yield
            att1["zero"] = POOL.put(pool_setup, over + [coef_free[0]],
                                    lambda: G.memset(near[:, :, 0:WINDOW], 0.0),
                                    lambda: G.memset(coef[:, :, :, :], 0.0))
            yield
            yield
            att1["w"] = split_small(w1, raw1, [raw_ready, *over])
            att1["over"] = over
            yield

        def side1(key, c):
            yield from layer_norm(key, c, x1_ready[c])
            buf = key % 2
            xt = (xnT[:, buf, 0], xnT[:, buf, 1])

            def w(lo, hi):
                return (w1[:, 0, lo:hi], w1[:, 1, lo:hi])

            def rows(r):
                return (xt[0][:, r * P:(r + 1) * P], xt[1][:, r * P:(r + 1) * P])

            ready = [xnT_ready[key], att1["w"]]
            over = att1["over"]
            b, ps = side_bank()
            mark = PE.put(pe_side, ready + [side_free[b]], *mm3(ps[:, :], w(0, P), xt))
            side_free[b] = SCAL.put(act_side, [mark, att1["in"], att1.get("qk_read"), *over],
                                    lambda ps=ps: A.activation(qT[:, :], ps[:, :], ACT.Identity, bias=b_q))
            yield
            b, ps = side_bank()
            mark = PE.put(pe_side, [side_free[b]], *mm3(ps[:, :], w(P, 2 * P), xt))
            side_free[b] = SCAL.put(act_side, [mark], lambda ps=ps: A.activation(kT[:, :], ps[:, :], ACT.Identity, bias=b_k))
            qk_ready = side_free[b]
            yield
            masked = []
            for s in range(SEQS):
                b, ps = side_bank()
                mark = PE.put(pe_side, [qk_ready, side_free[b]],
                              *[f for n, (at, width) in enumerate(KEYS) for f in
                                mm(ps[:, at:at + width], qT[:, s * SEQ + n * P:s * SEQ + (n + 1) * P], kT[:, s * SEQ:s * SEQ + width])])
                yield
                m = DVE.put(dve_side, [mark, att1["in"], att1["w"], att1.get("p_read")],
                            lambda ps=ps, s=s: V.tensor_tensor(scores[:, s], ps[:, 0:KEYCOLS], causal[:, :], ALU.add))
                side_free[b] = m
                masked.append(m)
            att1["qk_read"] = mark
            b, ps = side_bank()
            mark = PE.put(pe_side, [side_free[b]],
                          *[f for r in range(ROWS) for f in mm3(ps[:, r * P:(r + 1) * P], rows(r), w(2 * P, 3 * P))])
            yield
            v_ready = side_free[b] = SCAL.put(act_side, [mark, att1.get("v_read")], lambda ps=ps: A.copy(v1[:, :], ps[:, :]))
            place = [(s, at, width) for s in range(SEQS) for at, width in KEYS]
            m = DVE.put(dve_side, masked,
                        *[lambda r=r, s=s, at=at, wd=wd: V.max(best1[:, r], scores[:, s, at:at + wd]) for r, (s, at, wd) in enumerate(place)])
            b, ps_g = side_bank()
            g_mark = PE.put(pe_side, [side_free[b]],
                            *[f for r in range(ROWS) for f in mm3(ps_g[:, r * EXPERTS1:(r + 1) * EXPERTS1], rows(r), w(5 * P, 5 * P + EXPERTS1))])
            yield
            glog = ps_g[:, 0:ROWS * EXPERTS1].rearrange("p (r e) -> p r e", r=ROWS)
            g_max = DVE.put(dve_side, [g_mark], lambda: V.tensor_reduce(gsum[:, :], glog, axis=AX, op=ALU.max))
            by_e = [P, ROWS, EXPERTS1]
            g_sub = DVE.put(dve_side, [g_max], lambda: V.tensor_tensor(gate[:, :, :], glog, gsum[:, :].unsqueeze(2).to_broadcast(by_e), ALU.subtract))
            side_free[b] = g_sub
            scale = float(P) ** -0.5
            neg = DVE.put(dve_side, [m], lambda: V.tensor_scalar(top_neg[:, :], best1[:, :, 0], -scale, None, ALU.mult))
            m = DVE.put(dve_side, [m, *masked],
                        *[lambda r=r, s=s, at=at, wd=wd: V.match_replace(
                            out=rest[:, s, at:at + wd], in_to_replace=best1[:, r], in_values=scores[:, s, at:at + wd], imm_value=FAR)
                          for r, (s, at, wd) in enumerate(place)])
            yield
            b, ps = side_bank()
            mark = PE.put(pe_side, [side_free[b]], *mm3(ps[:, :], w(4 * P, 5 * P), xt))
            near_in = SCAL.put(act_side, [mark, att1["zero"], att1.get("near_read")], lambda ps=ps: A.copy(
                near[:, :, WINDOW:], ps[:, :].rearrange("p (s t) -> p s t", s=SEQS)))
            side_free[b] = near_in
            b, ps = side_bank()
            self_half = PE.put(pe_side, [side_free[b]], *mm3(ps[:, :], w(3 * P, 4 * P), xt))
            e_mark = SCAL.put(act_side, [m, neg],
                              *[lambda r=r, s=s, at=at, wd=wd, t=t: A.activation(
                                  t[:, s, at:at + wd], t[:, s, at:at + wd], ACT.Exp, bias=top_neg[:, r:r + 1], scale=scale)
                                for t in (scores, rest) for r, (s, at, wd) in enumerate(place)])
            g_exp = SCAL.put(act_side, [g_sub], lambda: A.activation(gate[:, :, :], gate[:, :, :], ACT.Exp))
            yield
            added = []
            seqs = lambda ap: ap.rearrange("p (s t) -> p s t", s=SEQS)
            heard = None
            msg_free = att1.get("msg_free", [None] * 3)
            for k in range(1, WINDOW + 1):
                slot = 0 if k == 1 else 1 + k % 2
                added = DVE.put(dve_side, [self_half, near_in, msg_free[slot]],
                                lambda ps=ps, k=k, slot=slot: V.tensor_tensor(
                                    seqs(msg[:, slot]), seqs(ps[:, :]), near[:, :, WINDOW - k:WINDOW - k + SEQ], ALU.add))
                if k > 1:
                    yield
                act = SCAL.put(act_side, [added], lambda slot=slot: A.activation(msg[:, slot], msg[:, slot], ACT.Silu, bias=b_m1))
                if k > 1:
                    heard = POOL.put(pool_side, [act, heard], lambda slot=slot: G.tensor_tensor(msg[:, 0], msg[:, 0], msg[:, slot], ALU.add))
                    msg_free[slot] = heard
            side_free[b] = added
            att1["near_read"] = added
            m = DVE.put(dve_side, [e_mark],
                        *[lambda r=r, s=s, at=at, wd=wd: V.scalar_tensor_tensor(
                            rest[:, s, at:at + wd], scores[:, s, at:at + wd], 1.0, rest[:, s, at:at + wd], ALU.mult, ALU.subtract,
                            accum_out=psum1[:, r:r + 1]) for r, (s, at, wd) in enumerate(place)])
            m = DVE.put(dve_side, [m], lambda: V.reciprocal(psum1[:, :], psum1[:, :]))
            yield
            m = DVE.put(dve_side, [m],
                        *[lambda r=r, s=s, at=at, wd=wd: V.tensor_scalar(
                            rest[:, s, at:at + wd], rest[:, s, at:at + wd], psum1[:, r:r + 1], None, ALU.mult)
                          for r, (s, at, wd) in enumerate(place)])
            yield
            for s in range(SEQS):
                b, ps = side_bank()
                mark = PE.put(pe_side, [m, side_free[b]],
                              *[lambda k=k, s=s, ps=ps: T.transpose(ps[:, k * P:(k + 1) * P], rest[:, s, k * P:(k + 1) * P], ident) for k in range(3)])
                pt = side_free[b] = SCAL.put(act_side, [mark], lambda ps=ps, s=s: A.copy(scores[:, s], ps[:, 0:KEYCOLS]))
                yield
            b, ps = side_bank()
            products = []
            for s in range(SEQS):
                v_a, v_b = (v1[:, r * P:(r + 1) * P] for r in (2 * s, 2 * s + 1))
                at = s * SEQ
                products += mm(ps[:, at:at + P], v_a, scores[:, s, 0:P])
                products += mm(ps[:, at + P:at + SEQ], v_a, scores[:, s, P:2 * P], stop=False)
                products += mm(ps[:, at + P:at + SEQ], v_b, scores[:, s, 2 * P:3 * P], start=False)
            mark = PE.put(pe_side, [pt, v_ready, side_free[b]], *products)
            att1["p_read"] = att1["v_read"] = mark
            yield
            glob = side_free[b] = SCAL.put(act_side, [mark, mix_free[0]], lambda ps=ps: A.activation(mix_b[:, :], ps[:, :], ACT.Identity, bias=b_v))
            b, ps = side_bank()
            mark = PE.put(pe_side, [heard, side_free[b]], *mm(ps[:, :], w_m2, msg[:, 0]))
            msg_free[0] = mark
            att1["msg_free"] = msg_free
            yield
            side_free[b] = SCAL.put(act_side, [mark, mix_free[0]], lambda ps=ps: A.activation(
                mix_a[:, :], ps[:, :], ACT.Identity, bias=b_m2, scale=1.0 / WINDOW))
            mix_ready[key] = side_free[b]
            g = DVE.chain(dve_side, [g_exp],
                          lambda: V.tensor_reduce(gsum[:, :], gate[:, :, :], axis=AX, op=ALU.add),
                          lambda: V.reciprocal(gsum[:, :], gsum[:, :]),
                          lambda: V.tensor_tensor(gate[:, :, :], gate[:, :, :], gsum[:, :].unsqueeze(2).to_broadcast(by_e), ALU.mult))
            yield
            g = rank_among_8(gate[:, :, :], ROWS, ga[:, :], gb[:, :], gsel[:, :, :], [g, common_ready])
            yield
            g = DVE.chain(dve_side, [g],
                          lambda: V.tensor_scalar(gsel[:, :, :], gsel[:, :, :], TOP1 - 0.5, None, ALU.is_lt),
                          lambda: V.tensor_tensor(gate[:, :, :], gate[:, :, :], gsel[:, :, :], ALU.mult),
                          lambda: V.tensor_reduce(gsum[:, :], gate[:, :, :], axis=AX, op=ALU.add),
                          lambda: V.reciprocal(gsum[:, :], gsum[:, :]),
                          lambda: V.tensor_tensor(gate[:, :, :], gate[:, :, :], gsum[:, :].unsqueeze(2).to_broadcast(by_e), ALU.mult))
            yield
            twice = [P, ROWS, EXPERTS1, 2]
            g = DVE.put(dve_side, [g, coef_free[0], att1["zero"]],
                        *[lambda n=n: V.tensor_copy(coef[:, :, n, 0:2 * EXPERTS1].rearrange("p r (e t) -> p r e t", t=2),
                                                    gate[:, :, :].unsqueeze(3).to_broadcast(twice)) for n in range(2)])
            yield
            yield from coef_to_columns(key, g)

        x1_ready = [None] * CHUNKS

        def finish(layer, c, y_mark):
            b, ps = side_bank()
            mark = PE.put(pe_side, [y_mark, side_free[b], common_ready],
                          *[lambda r=r: T.transpose(ps[:, r * P:(r + 1) * P], swing[:, r * P:(r + 1) * P], ident) for r in range(ROWS)])
            swing_free[0] = mark
            yield
            mark = DVE.put(dve_side, [mark], lambda: V.tensor_tensor(
                xres[:, c], ps[:, :].rearrange("p (r d) -> p r d", r=ROWS), xres[:, c], ALU.add))
            side_free[b] = mark
            x1_ready[c] = mark
            if layer == 1:
                SP.put(stored, [mark], lambda: nc.sync.dma_start(out_rows[c], xres[:, c]), by=16)
            yield

        tiles = [(0, c, j) for c in range(CHUNKS) for j in range(TILES0)] + \
                [(1, c, j) for c in range(CHUNKS) for j in range(TILES1)]
        hist = []

        def first_products(g):
            layer, c, j = tiles[g]
            key = c + layer * CHUNKS
            buf = key % 2
            xt = (xnT[:, buf, 0], xnT[:, buf, 1])
            w_gate, w_up, _ = tile_weights(j)
            m = {}
            two = hist[g - 2] if g >= 2 else {}
            split = list(w_split[j + layer * TILES0]) if c == 0 else []
            m["gate"] = PE.put(pe_gate, [xnT_ready[key], two.get("silu"), *split], *mm3(ps_gate[g % 2][:, :], w_gate, xt))
            m["up"] = PE.put(pe_up, [two.get("h1")], *mm3(ps_up[g % 2][:, :], w_up, xt))
            routed = not (layer == 0 and j == TILES0 - 1)
            pair = j if layer == 0 else j // 2
            if routed and (layer == 0 or j % 2 == 0):
                sel = pick_pair[:, pair % 2]
                picked = POOL.put(pool_pick, [common_ready, pick_free[pair % 2]],
                                  lambda: G.tensor_copy(sel, pick[:, 2 * pair:2 * pair + 2].unsqueeze(2).to_broadcast([P, 2, 64])))
                m["coef"] = PE.put(pe_coef, [coefT_ready[key], picked, coef_read[0]],
                                   *mm(ps_coef[:, :], sel.rearrange("p a b -> p (a b)"), coefT[:, buf]))
                coefT_free[buf] = pick_free[pair % 2] = m["coef"]
            else:
                m["coef"] = hist[g - 1]["coef"] if routed else None
            xnT_free[buf] = m["up"]
            hist.append(m)

        coef_read = [None]
        pick_free = [None, None]

        def times_coef(g):
            m = hist[g]
            s = g % 3
            if m["coef"] is None:
                m["h"] = m["h1"]
                return
            m["h"] = DVE.put(dve_coef, [m["h1"], m["coef"]],
                             lambda: V.tensor_tensor(silu_h[:, s], ps_coef[:, :], silu_h[:, s], ALU.mult))
            coef_read[0] = m["h"]

        def silu_and_up(g):
            m = hist[g]
            s = g % 3
            lo3 = hist[g - 3]["lo"] if g >= 3 else w0_ready
            m["silu"] = SCAL.put(act_silu, [m["gate"], lo3], lambda: A.activation(silu_h[:, s], ps_gate[g % 2][:, :], ACT.Silu))
            m["h1"] = DVE.put(dve_up, [m["silu"], m["up"]],
                              lambda: V.tensor_tensor(silu_h[:, s], ps_up[g % 2][:, :], silu_h[:, s], ALU.mult))

        def split_h(g):
            m = hist[g]
            s = g % 3
            down3 = hist[g - 3].get("down") if g >= 3 else None
            m["hi"] = SCAL.put(act_hi, [m["h"], down3], lambda: A.copy(h_hi[:, s], silu_h[:, s]))
            m["lo"] = POOL.put(pool_lo, [m["hi"], down3], lambda: G.tensor_tensor(h_lo[:, s], silu_h[:, s], f32(h_hi[:, s]), ALU.subtract))

        y_free = [None]

        def last_products(g):
            layer, c, j = tiles[g]
            m = hist[g]
            s = g % 3
            key = c + layer * CHUNKS
            _, _, w_down = tile_weights(j)
            last = j == (TILES1 if layer else TILES0) - 1
            if j == 0:
                if layer == 0:
                    terms = mm(ps_y[:, :], w_out[:, :], mix_a[:, :], stop=False)
                else:
                    terms = mm(ps_y[:, :], w_ol, mix_a[:, :], stop=False) + \
                        mm(ps_y[:, :], w_og, mix_b[:, :], start=False, stop=False)
                mix_free[0] = PE.put(pe_side, [mix_ready[key], y_free[0], att0_ready if layer == 0 else att1["in"]], *terms)
            m["down"] = PE.put(pe_down, [m["hi"], m["lo"]], *mm3(ps_y[:, :], w_down, (h_hi[:, s], h_lo[:, s]), start=False, stop=last))
            if last:
                bias = b_o if layer else None
                copy = (lambda: A.activation(swing[:, :], ps_y[:, :], ACT.Identity, bias=bias)) if layer else \
                    (lambda: A.copy(swing[:, :], ps_y[:, :]))
                y_free[0] = SCAL.put(act_y, [m["down"], swing_free[0]], copy)
                swing_free[0] = y_free[0]
                return finish(layer, c, y_free[0])
            return None

        def drain(steps):
            for _ in steps:
                pass

        AHEAD = 3
        for j in range(AHEAD):
            split_tile(0, j)
        drain(side0(0, 0))

        side = iter(())
        for g, (layer, c, j) in enumerate(tiles):
            done = None
            if g >= LAG:
                done = last_products(g - LAG)
            if done is not None:
                closing = [done]
            elif j < LAG:
                closing = []
            if g >= 1:
                times_coef(g - 1)
            first_products(g)
            silu_and_up(g)
            if g >= 1:
                split_h(g - 1)
            if layer == 0 and c == 0 and j + AHEAD < TILES0:
                split_tile(0, j + AHEAD)
            if layer == 0 and c == CHUNKS - 1:
                k = j - LAG - 1
                if 0 <= k < TILES1:
                    split_tile(1, k, free=[hist[g - LAG - 1]["down"]])
            if layer == 0 and c == 0 and j == TILES0 - 1:
                for cc in range(3, CHUNKS):
                    x_ready[cc] = load(x_in[cc], xres[:, cc], x_rows[cc])
            if j == LAG:
                def steps(layer=layer, c=c, closing=closing):
                    for one in closing:
                        yield from one
                    if layer == 0 and c < CHUNKS - 1:
                        yield from side0(c + 1, c + 1)
                    elif layer == 0:
                        yield from side1_setup()
                        yield from side1(CHUNKS, 0)
                    elif c < CHUNKS - 1:
                        yield from side1(CHUNKS + c + 1, c + 1)
                side = steps()
            n_tiles = TILES1 if layer else TILES0
            left = n_tiles - 1 - j
            if j >= LAG:
                for _ in range(4 if layer else 2):
                    next(side, None)
                if left == 0:
                    drain(side)
        n = len(tiles)
        for k in range(3):
            if k == 0:
                times_coef(n - 1)
                split_h(n - 1)
            done = last_products(n - LAG + k)
        drain(done)
        SP_last = (stored, stored.n)

        block = ctx.enter_context(nc.Block())

        @block.sync
        def _(eng):
            SP.run(eng)
            eng.wait_ge(SP_last[0].sem, SP_last[1])

        @block.tensor
        def _(eng):
            PE.run(eng)

        @block.vector
        def _(eng):
            DVE.run(eng)

        @block.scalar
        def _(eng):
            SCAL.run(eng)

        @block.gpsimd
        def _(eng):
            POOL.run(eng)


def shape_constants():
    ident = np.eye(P, dtype=np.float32)
    pick = (np.arange(P)[:, None] % 64 == np.arange(64)[None, :]).astype(np.float32)
    earlier = np.broadcast_to((np.arange(8)[None, :] < np.arange(8)[:, None]).astype(np.float32).reshape(1, 64), (P, 64))
    common = np.concatenate([ident, pick, earlier], 1)
    head = np.arange(P) // HEAD
    same_head = (head[:, None] == head[None, :]).astype(np.float32)
    inv_freq = (np.float32(1.0) / np.float32(ROPE_BASE) ** (np.arange(0, HEAD, 2, dtype=np.float32) / np.float32(HEAD))).astype(np.float32)
    freqs = np.arange(SEQ, dtype=np.float32)[:, None] * inv_freq[None, :]
    angle = np.tile(np.concatenate([freqs, freqs], 1), (1, HEADS))
    cos, sin = np.cos(angle), np.sin(angle)
    sign = np.where(np.arange(P) % HEAD < HEAD // 2, -1.0, 1.0).astype(np.float32)
    sin = sin * sign[None, :]
    scale = np.float32(HEAD ** -0.5)
    by_row = lambda t: t.reshape(2, P, P).transpose(1, 0, 2).reshape(P, SEQ)
    att0 = np.concatenate([same_head, cos.T * scale, sin.T * scale, by_row(cos), by_row(sin)], 1)
    tri = np.where(np.arange(P)[None, :] > np.arange(P)[:, None], FAR, 0.0)
    att1 = np.concatenate([tri, np.zeros((P, P)), tri], 1)
    return tuple(np.ascontiguousarray(t.astype(np.float32)) for t in (common, att0, att1))


def kernel(**inputs):
    import concourse.bacc as bacc
    from concourse.bass_utils import run_bass_kernel_spmd

    a = {k: np.asarray(v) for k, v in inputs.items()}
    cat = np.concatenate
    common_c, att0_c, att1_c = shape_constants()

    pairs = EXPERTS0 * FF0 // P

    def paired(w):
        return w.reshape(pairs, 2, P, FF0).transpose(0, 2, 1, 3).reshape(pairs, P, P)

    tiles0 = cat([paired(a["L0_ffn_Wg"]), paired(a["L0_ffn_Wu"]), a["L0_ffn_Wd"].reshape(pairs, P, P)], 2)
    shared = cat([a["L0_ffn_SWg"], a["L0_ffn_SWu"], a["L0_ffn_SWd"]], 1)[None]

    def halves(w):
        return w.reshape(TILES1, P, P).transpose(0, 2, 1)

    down1 = a["L1_ffn_w2"].reshape(EXPERTS1, P, 2, P).transpose(0, 2, 3, 1).reshape(TILES1, P, P)
    tiles1 = cat([halves(a["L1_ffn_w1"]), halves(a["L1_ffn_w3"]), down1], 2)
    ffn_w = cat([tiles0, shared, tiles1], 0)
    wq, wk, wv = np.split(a["L0_attn_W_qkv"], 3, axis=1)
    swap = (np.arange(P) // HEAD) * HEAD + (np.arange(P) % HEAD + HEAD // 2) % HEAD
    att0_w = cat([wq, wq[:, swap], wk, wk[:, swap], wv, a["L0_ffn_router_w"].T], 1)
    wm1, wo = a["L1_attn_Wm1"], a["L1_attn_Wo"]
    att1_w = cat([a["L1_attn_Wq"], a["L1_attn_Wk"], a["L1_attn_Wv"], wm1[:P], wm1[P:], a["L1_ffn_gate_w"].T], 1)
    att1_f = cat([a["L1_attn_Wm2"], wo[:P], wo[P:]], 1)
    att1_b = np.stack([a[f"L1_attn_{n}"] for n in ("bq", "bk", "bv", "bm1", "bm2", "bo")], 1)
    arrays = {
        "x": a["L0_attn_x"].reshape(TOKENS, P), "ffn_w": ffn_w, "att0_w": att0_w, "att0_f": a["L0_attn_W_out"],
        "att0_c": att0_c, "e_bias": a["L0_ffn_e_bias"], "att1_w": att1_w, "att1_f": att1_f, "att1_b": att1_b,
        "att1_c": att1_c, "common_c": common_c,
    }
    arrays = {k: np.ascontiguousarray(v) for k, v in arrays.items()}
    nc = bacc.Bacc("TRN2", target_bir_lowering=False, num_devices=1)
    args = [nc.dram_tensor(f"in_{k}", v.shape, mybir.dt.from_np(v.dtype), kind="ExternalInput").ap() for k, v in arrays.items()]
    out = nc.dram_tensor("out", (TOKENS, P), FP32, kind="ExternalOutput").ap()
    build_program(nc, *args, out)
    r = run_bass_kernel_spmd(nc, [{f"in_{k}": v for k, v in arrays.items()}], core_ids=[0])
    return r.results[0]["out"].reshape(a["L0_attn_x"].shape)
```

```python
from contextlib import ExitStack

import concourse.bass as bass
import numpy as np
from concourse import mybir

FP32 = mybir.dt.float32
FP32R = mybir.dt.float32r
ALU = mybir.AluOpType
ACT = mybir.ActivationFunctionType
AX = mybir.AxisListType.X

P = 128
SEQ = 256
TOKENS = 32 * SEQ
CHUNK = 512
ROWS = CHUNK // P
SEQS = CHUNK // SEQ
CHUNKS = TOKENS // CHUNK
HEADS, HEAD = 16, 8
ROPE_BASE = 500000.0
EXPERTS0, FF0, GROUPS0, TOP_GROUPS0, TOP0, SCALE0 = 64, 64, 8, 4, 8, 2.5
EXPERTS1, FF1, TOP1 = 8, 256, 2
WINDOW, TOP_KEYS = 4, 8
TILES0 = EXPERTS0 * FF0 // P + 1
TILES1 = EXPERTS1 * FF1 // P
FAR = -1.0e30
EPS_LN, EPS_DEN, EPS_W = 1e-5, 1e-6, 1e-20
KEYS = [(0, P), (P, SEQ)]
KEYCOLS = P + SEQ
STAGES_W = 3
LAG = 3
EXP = "exp"


class Stage:

    def __init__(self, sem):
        self.sem, self.n = sem, 0

    def done(self, by=1):
        self.n += by
        return (self, self.n)


class Line:

    def __init__(self):
        self.items, self.seen = [], {}

    def put(self, stage, waits, *instructions, by=1):
        need = []
        for mark in waits:
            if mark is not None and self.seen.get(mark[0], 0) < mark[1]:
                self.seen[mark[0]] = mark[1]
                need.append(mark)
        mark = stage.done(by)
        self.items.append((need, instructions, stage, by))
        return mark

    def chain(self, stage, waits, *instructions):
        mark = None
        for n, one in enumerate(instructions):
            mark = self.put(stage, waits if n == 0 else [mark], one)
        return mark

    def run(self, engine):
        for need, instructions, stage, by in self.items:
            for sem_stage, value in need:
                engine.wait_ge(sem_stage.sem, value)
            for one in instructions:
                last = one()
            last.then_inc(stage.sem, by)


def build_program(nc, x, ffn_w, att0_w, att0_f, att0_c, e_bias, att1_w, att1_f, att1_b, att1_c, common_c, out):
    ctx = ExitStack()
    with ctx:
        def sb(name, shape, dtype=FP32, within=ctx):
            return within.enter_context(nc.sbuf_tensor(name, [P] + list(shape), dtype))

        def stage(name):
            return Stage(ctx.enter_context(nc.semaphore(name)))

        xres = sb("xres", [CHUNKS, ROWS, P])
        w_gu = sb("w_gu", [TILES0, 2, 2, P], FP32R)
        w_dn = sb("w_dn", [TILES0, 2, P], FP32R)
        w_raw = sb("w_raw", [STAGES_W, 3, P])
        xnT = sb("xnT", [2, 2, CHUNK], FP32R)
        coefT = sb("coefT", [2, CHUNK], FP32R)
        coef = sb("coef", [ROWS, 2, 64])
        silu_h = sb("silu_h", [3, CHUNK])
        h_hi = sb("h_hi", [3, CHUNK], FP32R)
        h_lo = sb("h_lo", [3, CHUNK], FP32R)
        swing = sb("swing", [CHUNK])
        mix_a = sb("mix_a", [CHUNK])
        mix_b = sb("mix_b", [CHUNK])
        common = sb("common", [P + 64 + 64])
        ident, pick, earlier = common[:, 0:P], common[:, P:P + 64], common[:, P + 64:P + 128]
        w_out = sb("w_out", [P])
        pick_pair = sb("pick_pair", [2, 2, 64], FP32R)
        stats = sb("stats", [ROWS, 6])
        mean_var = sb("mean_var", [ROWS, 2])
        rstd = sb("rstd", [ROWS])
        minus_half = sb("minus_half", [ROWS])

        in0 = ExitStack()
        c0 = sb("att0_const", [P + 4 * SEQ], within=in0)
        same_head = c0[:, 0:P]
        cosq, sinq, cosk, sink = (c0[:, P + n * SEQ:P + (n + 1) * SEQ] for n in range(4))
        w0 = sb("w0", [2, 5 * P + EXPERTS0], FP32R, within=in0)
        bias0 = sb("bias0", [EXPERTS0], within=in0)
        ones = sb("ones", [P], within=in0)
        kf = sb("kf", [CHUNK], within=in0)
        qf = sb("qf", [CHUNK], within=in0)
        tmp0 = sb("tmp0", [CHUNK], within=in0)
        v0 = sb("v0", [CHUNK], within=in0)
        kv = sb("kv", [SEQS, 2, P], within=in0)
        score0 = sb("score0", [ROWS * EXPERTS0], within=in0)
        sfc = sb("sfc", [ROWS * EXPERTS0], within=in0)
        ra = sb("ra", [ROWS * 64], within=in0)
        rb = sb("rb", [ROWS * 64], within=in0)
        hi4 = sb("hi4", [ROWS * GROUPS0, 4], within=in0)
        lo4 = sb("lo4", [ROWS * GROUPS0, 4], within=in0)
        hi2 = sb("hi2", [ROWS * GROUPS0, 2], within=in0)
        mi2 = sb("mi2", [ROWS * GROUPS0, 2], within=in0)
        lo2 = sb("lo2", [ROWS * GROUPS0, 2], within=in0)
        g_a = sb("g_a", [ROWS * GROUPS0], within=in0)
        g_b = sb("g_b", [ROWS * GROUPS0], within=in0)
        best0 = sb("best0", [ROWS, 8], within=in0)
        wsum0 = sb("wsum0", [ROWS], within=in0)
        in0.close()

        in1 = ExitStack()
        causal = sb("causal", [KEYCOLS], within=in1)
        w1 = sb("w1", [2, 5 * P + EXPERTS1], FP32R, within=in1)
        f1 = sb("f1", [3 * P], within=in1)
        w_m2, w_ol, w_og = (f1[:, n * P:(n + 1) * P] for n in range(3))
        b1 = sb("b1", [6], within=in1)
        b_q, b_k, b_v, b_m1, b_m2, b_o = (b1[:, n:n + 1] for n in range(6))
        qT = sb("qT", [CHUNK], within=in1)
        kT = sb("kT", [CHUNK], within=in1)
        v1 = sb("v1", [CHUNK], within=in1)
        scores = sb("scores", [SEQS, KEYCOLS], within=in1)
        rest = sb("rest", [SEQS, KEYCOLS], within=in1)
        near = sb("near", [SEQS, WINDOW + SEQ], within=in1)
        msg = sb("msg", [3, CHUNK], within=in1)
        best1 = sb("best1", [ROWS, 8], within=in1)
        top_neg = sb("top_neg", [ROWS], within=in1)
        psum1 = sb("psum1", [ROWS], within=in1)
        gate = sb("gate", [ROWS, EXPERTS1], within=in1)
        gsel = sb("gsel", [ROWS, EXPERTS1], within=in1)
        ga = sb("ga", [ROWS * 64], within=in1)
        gb = sb("gb", [ROWS * 64], within=in1)
        gsum = sb("gsum", [ROWS], within=in1)
        in1.close()

        def bank(name):
            return ctx.enter_context(nc.psum_tensor(name, [P, CHUNK], FP32))

        ps_gate = [bank("ps_gate0"), bank("ps_gate1")]
        ps_up = [bank("ps_up0"), bank("ps_up1")]
        ps_coef = bank("ps_coef")
        ps_y = bank("ps_y")
        ps_side = [bank("ps_side0"), bank("ps_side1")]

        x_in = [stage(f"x_in{c}") for c in range(CHUNKS)]
        w_in = [stage(f"w_in{n}") for n in range(STAGES_W)]
        const_in = stage("const_in")
        att0_in = stage("att0_in")
        att1_in = stage("att1_in")
        att1_raw_in = stage("att1_raw_in")
        stored = stage("stored")
        pe_gate, pe_up, pe_coef, pe_down, pe_mix = (stage(n) for n in ("pe_gate", "pe_up", "pe_coef", "pe_down", "pe_mix"))
        act_silu, act_hi, act_whi, act_y = (stage(n) for n in ("act_silu", "act_hi", "act_whi", "act_y"))
        dve_up, dve_coef, dve_wlo = (stage(n) for n in ("dve_up", "dve_coef", "dve_wlo"))
        pool_lo, dve_pick = stage("pool_lo"), stage("dve_pick")
        pe_side, act_side, dve_side, pool_side = (stage(n) for n in ("pe_side", "act_side", "dve_side", "pool_side"))
        dve_setup, pool_setup, act_setup = stage("dve_setup"), stage("pool_setup"), stage("act_setup")

        PE, SCAL, DVE, POOL, SP = (Line() for _ in range(5))
        T, A, V, G = nc.tensor, nc.scalar, nc.vector, nc.gpsimd

        def f32(ap):
            return ap.bitcast(FP32)

        def mm3(dst, w, m, start=True, stop=True):
            return [lambda: T.matmul(dst, w[0], m[0], start=start, stop=False),
                    lambda: T.matmul(dst, w[1], m[0], start=False, stop=False),
                    lambda: T.matmul(dst, w[0], m[1], start=False, stop=stop)]

        def mm(dst, w, m, start=True, stop=True):
            return [lambda: T.matmul(dst, w, m, start=start, stop=stop)]

        def load(stg, dst, src):
            return SP.put(stg, [], lambda: nc.sync.dma_start(dst, src), by=16)

        x_rows = x.rearrange("(c r p) d -> c p r d", r=ROWS, p=P)
        out_rows = out.rearrange("(c r p) d -> c p r d", r=ROWS, p=P)
        raw0 = silu_h[:, :, :].rearrange("p a b -> p (a b)")[:, 0:5 * P + EXPERTS0]
        x_ready = [None] * CHUNKS
        x_ready[0] = load(x_in[0], xres[:, 0], x_rows[0])
        common_ready = load(const_in, common[:, :], common_c)
        load(att0_in, raw0, att0_w)
        load(att0_in, c0[:, :], att0_c)
        load(att0_in, w_out[:, :], att0_f)
        att0_ready = load(att0_in, bias0[:, :], e_bias.partition_broadcast(P))

        w_split = [None] * (TILES0 + TILES1)
        w_loaded = [None] * (TILES0 + TILES1)

        def load_tile(n):
            waits = list(w_split[n - STAGES_W]) if n >= STAGES_W else []
            w_loaded[n] = SP.put(w_in[n % STAGES_W], waits,
                                 lambda: nc.sync.dma_start(w_raw[:, n % STAGES_W], ffn_w[n].rearrange("p (k d) -> p k d", k=3)), by=16)

        for n in range(STAGES_W):
            load_tile(n)
        for c in range(1, min(3, CHUNKS)):
            x_ready[c] = load(x_in[c], xres[:, c], x_rows[c])

        def tile_weights(j):
            gu, dn = w_gu[:, j], w_dn[:, j]
            return (gu[:, 0, 0], gu[:, 0, 1]), (gu[:, 1, 0], gu[:, 1, 1]), (dn[:, 0], dn[:, 1])

        def split_tile(layer, j, free=()):
            n = j + layer * TILES0
            raw = w_raw[:, n % STAGES_W]
            gu, dn = w_gu[:, j], w_dn[:, j]
            hi = SCAL.put(act_whi, [w_loaded[n], *free],
                          lambda: A.copy(gu[:, :, 0], raw[:, 0:2]),
                          lambda: A.copy(dn[:, 0], raw[:, 2]))
            lo = DVE.put(dve_wlo, [hi],
                         lambda: V.tensor_tensor(gu[:, :, 1], raw[:, 0:2], f32(gu[:, :, 0]), ALU.subtract),
                         lambda: V.tensor_tensor(dn[:, 1], raw[:, 2], f32(dn[:, 0]), ALU.subtract))
            w_split[n] = (hi, lo)
            if n + STAGES_W < TILES0 + TILES1:
                load_tile(n + STAGES_W)

        pow_ready = DVE.put(dve_setup, [], lambda: V.memset(minus_half[:, :], -0.5))
        ones_ready = DVE.put(dve_setup, [], lambda: V.memset(ones[:, :], 1.0))

        def split_small(dst, raw, waits):
            hi = SCAL.put(act_setup, waits, lambda: A.copy(dst[:, 0], raw))
            return DVE.put(dve_setup, [hi], lambda: V.tensor_tensor(dst[:, 1], raw, f32(dst[:, 0]), ALU.subtract))

        w0_ready = split_small(w0, raw0, [att0_ready])

        free_banks = [(0, w0_ready), (1, w0_ready)]

        def take():
            while not free_banks:
                yield
            n, mark = free_banks.pop(0)
            return n, ps_side[n], mark

        def give(n, mark):
            free_banks.append((n, mark))

        xnT_free = [None, None]
        coefT_free = [None, None]
        swing_free = [None]
        xnT_ready, coefT_ready, mix_ready = {}, {}, {}
        mix_free = [None]
        score_free = [None]
        coef_free = [None]

        def layer_norm(key, c, x_mark):
            buf = key % 2
            mark = DVE.put(dve_side, [x_mark],
                           *[lambda r=r: V.bn_stats(stats[:, r], xres[:, c, r]) for r in range(ROWS)])
            mark = DVE.put(dve_side, [mark],
                           *[lambda r=r: V.bn_aggr(mean_var[:, r], stats[:, r]) for r in range(ROWS)])
            mark = DVE.put(dve_side, [mark], lambda: V.tensor_scalar(rstd[:, :], mean_var[:, :, 1], EPS_LN, None, ALU.add))
            yield
            mark = POOL.put(pool_side, [mark, pow_ready],
                            lambda: G.tensor_tensor(rstd[:, :], rstd[:, :], minus_half[:, :], ALU.pow))
            yield
            mark = DVE.put(dve_side, [mark, swing_free[0]],
                           *[lambda r=r: V.tensor_scalar(swing[:, r * P:(r + 1) * P], xres[:, c, r], mean_var[:, r, 0:1],
                                                         rstd[:, r:r + 1], ALU.subtract, ALU.mult) for r in range(ROWS)])
            yield
            b, ps, free = yield from take()
            mark = PE.put(pe_side, [mark, free, common_ready],
                          *[lambda r=r: T.transpose(ps[:, r * P:(r + 1) * P], swing[:, r * P:(r + 1) * P], ident)
                            for r in range(ROWS)])
            swing_free[0] = mark
            yield
            hi = SCAL.put(act_side, [mark, xnT_free[buf]], lambda: A.copy(xnT[:, buf, 0], ps[:, :]))
            yield
            lo = DVE.put(dve_side, [hi], lambda: V.tensor_tensor(xnT[:, buf, 1], ps[:, :], f32(xnT[:, buf, 0]), ALU.subtract))
            give(b, lo)
            xnT_ready[key] = lo
            yield

        def rank_among_8(values, rows, above, equal, count, waits):
            shape = [P, rows, 8, 8]
            mine = values.unsqueeze(3).to_broadcast(shape)
            other = values.unsqueeze(2).to_broadcast(shape)
            first = earlier.rearrange("p (g h) -> p g h", g=8).unsqueeze(1).to_broadcast(shape)
            ab = above.rearrange("p (r g h) -> p r g h", g=8, h=8)
            eq = equal.rearrange("p (r g h) -> p r g h", g=8, h=8)
            m = DVE.put(dve_side, waits, lambda: V.tensor_tensor(ab, other, mine, ALU.is_gt),
                        lambda: V.tensor_tensor(eq, other, mine, ALU.is_equal))
            yield
            return DVE.chain(dve_side, [m],
                             lambda: V.tensor_tensor(eq, eq, first, ALU.mult),
                             lambda: V.tensor_tensor(above, above, equal, ALU.add),
                             lambda: V.tensor_reduce(count, ab, axis=AX, op=ALU.add))

        def coef_to_columns(key, mark):
            buf = key % 2
            b, ps, free = yield from take()
            flat = coef[:, :, :, :].rearrange("p r a e -> p r (a e)")
            mark = PE.put(pe_side, [mark, free],
                          *[lambda r=r: T.transpose(ps[:, r * P:(r + 1) * P], flat[:, r], ident) for r in range(ROWS)])
            coef_free[0] = mark
            yield
            hi = SCAL.put(act_side, [mark, coefT_free[buf]], lambda: A.copy(coefT[:, buf], ps[:, :]))
            yield
            lo = DVE.put(dve_side, [hi], lambda: V.tensor_tensor(coefT[64:P, buf], ps[64:P, :], f32(coefT[64:P, buf]), ALU.subtract))
            give(b, lo)
            coefT_ready[key] = lo
            yield

        def columns_and_rows(key):
            buf = key % 2
            whole = (xnT[:, buf, 0], xnT[:, buf, 1])
            return whole, [(whole[0][:, r * P:(r + 1) * P], whole[1][:, r * P:(r + 1) * P]) for r in range(ROWS)]

        def seqs(ap):
            return ap.rearrange("p (s t) -> p s t", s=SEQS)

        att0_last = [None]

        def attention0(key, c):
            xt, rows = columns_and_rows(key)

            def w(lo, hi):
                return (w0[:, 0, lo:hi], w0[:, 1, lo:hi])

            for r in range(ROWS):
                b, ps, free = yield from take()
                mark = PE.put(pe_side, [xnT_ready[key], w0_ready, free, mix_free[0]], *mm3(ps[:, 0:3 * P], rows[r], w(2 * P, 5 * P)))
                yield
                half = (r % 2) * P
                DVE.put(dve_side, [mark],
                        lambda ps=ps, r=r, half=half: V.tensor_tensor(kf[:, r * P:(r + 1) * P], ps[:, 0:P], cosk[:, half:half + P], ALU.mult))
                k_parts = DVE.put(dve_side, [mark],
                                  lambda ps=ps, r=r, half=half: V.tensor_tensor(tmp0[:, r * P:(r + 1) * P], ps[:, P:2 * P], sink[:, half:half + P], ALU.mult))
                v_ready = SCAL.put(act_side, [k_parts], lambda ps=ps, r=r: A.copy(v0[:, r * P:(r + 1) * P], ps[:, 2 * P:3 * P]))
                give(b, v_ready)
            k_rope = POOL.put(pool_side, [k_parts], lambda: G.tensor_tensor(kf[:, :], kf[:, :], tmp0[:, :], ALU.add))
            yield
            by_seq = [P, SEQS, SEQ]
            b, ps, free = yield from take()
            mark = PE.put(pe_side, [free], *mm3(ps[:, :], w(0, P), xt))
            yield
            mark = DVE.put(dve_side, [mark], lambda ps=ps: V.tensor_tensor(
                seqs(qf[:, :]), seqs(ps[:, :]), cosq.unsqueeze(1).to_broadcast(by_seq), ALU.mult))
            give(b, mark)
            b, ps, free = yield from take()
            mark = PE.put(pe_side, [free], *mm3(ps[:, :], w(P, 2 * P), xt))
            yield
            mark = DVE.put(dve_side, [mark, k_rope], lambda ps=ps: V.tensor_tensor(
                seqs(tmp0[:, :]), seqs(ps[:, :]), sinq.unsqueeze(1).to_broadcast(by_seq), ALU.mult))
            give(b, mark)
            q_rope = POOL.put(pool_side, [mark], lambda: G.tensor_tensor(qf[:, :], qf[:, :], tmp0[:, :], ALU.add))
            yield
            k_min = DVE.put(dve_side, [k_rope], lambda: V.tensor_scalar(mix_b[:, :], kf[:, :], 0.0, None, ALU.min))
            yield
            q_min = DVE.put(dve_side, [q_rope], lambda: V.tensor_scalar(tmp0[:, :], qf[:, :], 0.0, None, ALU.min))
            yield EXP
            k_exp = SCAL.put(act_side, [k_min], lambda: A.activation(mix_b[:, :], mix_b[:, :], ACT.Exp))
            q_exp = SCAL.put(act_side, [q_min], lambda: A.activation(tmp0[:, :], tmp0[:, :], ACT.Exp))
            yield
            kf_ready = DVE.put(dve_side, [k_exp], lambda: V.scalar_tensor_tensor(kf[:, :], kf[:, :], 0.0, mix_b[:, :], ALU.max, ALU.add))
            yield
            qf_ready = DVE.put(dve_side, [q_exp], lambda: V.scalar_tensor_tensor(qf[:, :], qf[:, :], 0.0, tmp0[:, :], ALU.max, ALU.add))
            b, ps, free = yield from take()
            k_sum = SEQS * P
            products = []
            for s in range(SEQS):
                for at, n, rhs in ((s * P, P, lambda r: v0[:, r * P:(r + 1) * P]), (k_sum + s, 1, lambda r: ones[:, 0:1])):
                    for r in (2 * s, 2 * s + 1):
                        products += mm(ps[:, at:at + n], kf[:, r * P:(r + 1) * P], rhs(r), start=r == 2 * s, stop=r == 2 * s + 1)
            mark = PE.put(pe_side, [kf_ready, v_ready, ones_ready, free], *products)
            yield
            kv_ready = DVE.put(dve_side, [mark],
                               lambda ps=ps: V.tensor_tensor(
                                   kv[:, :, 0], ps[:, 0:k_sum].rearrange("p (s d) -> p s d", s=SEQS),
                                   same_head.unsqueeze(1).to_broadcast([P, SEQS, P]), ALU.mult),
                               *[lambda ps=ps, s=s: V.tensor_scalar(kv[:, s, 1], same_head, ps[:, k_sum + s:k_sum + s + 1], None, ALU.mult)
                                 for s in range(SEQS)])
            give(b, kv_ready)
            yield

            def against_q(n, ps):
                return [f for s in range(SEQS) for f in mm(ps[:, s * SEQ:(s + 1) * SEQ], kv[:, s, n], qf[:, s * SEQ:(s + 1) * SEQ])]

            b, ps, free = yield from take()
            mark = PE.put(pe_side, [kv_ready, qf_ready, free], *against_q(1, ps))
            yield
            mark = DVE.put(dve_side, [mark], lambda ps=ps: V.tensor_scalar(tmp0[:, :], ps[:, :], EPS_DEN, None, ALU.max))
            give(b, mark)
            b, ps, free = yield from take()
            numerator = PE.put(pe_side, [free], *against_q(0, ps))
            yield
            inverse = []
            for r in range(ROWS):
                inverse.append(DVE.put(dve_side, [mark], lambda r=r: V.reciprocal(tmp0[:, r * P:(r + 1) * P], tmp0[:, r * P:(r + 1) * P])))
                yield
            mark = DVE.put(dve_side, [numerator, *inverse], lambda ps=ps: V.tensor_tensor(mix_a[:, :], ps[:, :], tmp0[:, :], ALU.mult))
            give(b, mark)
            mix_ready[key] = mark
            yield

        def routing0(key, c):
            yield from layer_norm(key, c, x_ready[c])
            _, rows = columns_and_rows(key)
            b, ps, free = yield from take()
            mark = PE.put(pe_side, [xnT_ready[key], w0_ready, free],
                          *[f for r in range(ROWS) for f in
                            mm3(ps[:, r * EXPERTS0:(r + 1) * EXPERTS0], rows[r], (w0[:, 0, 5 * P:], w0[:, 1, 5 * P:]))])
            yield EXP
            mark = SCAL.put(act_side, [mark, score_free[0]], lambda: A.activation(score0[:, :], ps[:, 0:ROWS * EXPERTS0], ACT.Exp, scale=-1.0))
            give(b, mark)
            yield
            score = DVE.put(dve_side, [mark], lambda: V.tensor_scalar(score0[:, :], score0[:, :], 1.0, None, ALU.add))
            half = ROWS * EXPERTS0 // 2
            for n in range(2):
                part = score0[:, n * half:(n + 1) * half]
                yield
                score2 = DVE.put(dve_side, [score], lambda part=part: V.reciprocal(part, part))
            by_tok = [P, ROWS, EXPERTS0]
            row = lambda ap: ap.rearrange("p (r e) -> p r e", r=ROWS)
            choice = DVE.put(dve_side, [score2], lambda: V.tensor_tensor(
                row(sfc[:, :]), row(score0[:, :]), bias0[:, :].unsqueeze(1).to_broadcast(by_tok), ALU.add))
            yield
            grp = sfc[:, :].rearrange("p (g e) -> p g e", e=8)
            m = DVE.put(dve_side, [choice],
                        lambda: V.tensor_tensor(hi4[:, :, :], grp[:, :, 0:4], grp[:, :, 4:8], ALU.max),
                        lambda: V.tensor_tensor(lo4[:, :, :], grp[:, :, 0:4], grp[:, :, 4:8], ALU.min))
            yield
            m = DVE.put(dve_side, [m],
                        lambda: V.tensor_tensor(hi2[:, :, :], hi4[:, :, 0:2], hi4[:, :, 2:4], ALU.max),
                        lambda: V.tensor_tensor(mi2[:, :, :], hi4[:, :, 0:2], hi4[:, :, 2:4], ALU.min),
                        lambda: V.tensor_tensor(lo2[:, :, :], lo4[:, :, 0:2], lo4[:, :, 2:4], ALU.max))
            m = DVE.put(dve_side, [m], lambda: V.tensor_tensor(lo2[:, :, :], lo2[:, :, :], mi2[:, :, :], ALU.max))
            yield
            m = DVE.put(dve_side, [m],
                        lambda: V.tensor_tensor(mi2[:, :, 0], hi2[:, :, 0], hi2[:, :, 1], ALU.min),
                        lambda: V.tensor_tensor(g_a[:, :], hi2[:, :, 0], hi2[:, :, 1], ALU.max),
                        lambda: V.tensor_tensor(lo2[:, :, 0], lo2[:, :, 0], lo2[:, :, 1], ALU.max))
            m = DVE.chain(dve_side, [m],
                          lambda: V.tensor_tensor(lo2[:, :, 0], lo2[:, :, 0], mi2[:, :, 0], ALU.max),
                          lambda: V.tensor_tensor(g_a[:, :], g_a[:, :], lo2[:, :, 0], ALU.add))
            yield
            m = yield from rank_among_8(g_a[:, :].rearrange("p (r g) -> p r g", r=ROWS), ROWS, ra[:, :], rb[:, :],
                                        g_b[:, :].rearrange("p (r g) -> p r g", r=ROWS), [m, common_ready])
            yield
            m = DVE.chain(dve_side, [m],
                          lambda: V.tensor_scalar(g_b[:, :], g_b[:, :], TOP_GROUPS0 - 0.5, None, ALU.is_lt),
                          lambda: V.tensor_tensor(grp, grp, g_b[:, :].unsqueeze(2).to_broadcast([P, ROWS * GROUPS0, 8]), ALU.mult),
                          lambda: V.tensor_scalar(sfc[:, :], sfc[:, :], 0.0, None, ALU.add))
            yield
            m = DVE.put(dve_side, [m], *[lambda r=r: V.max(best0[:, r], row(sfc[:, :])[:, r]) for r in range(ROWS)])
            yield
            m = DVE.put(dve_side, [m], *[lambda r=r: V.match_replace(
                out=row(ra[:, :])[:, r], in_to_replace=best0[:, r], in_values=row(sfc[:, :])[:, r], imm_value=FAR) for r in range(ROWS)])
            yield
            m = DVE.chain(dve_side, [m],
                          lambda: V.tensor_tensor(ra[:, :], ra[:, :], sfc[:, :], ALU.not_equal),
                          lambda: V.tensor_tensor(ra[:, :], ra[:, :], score0[:, :], ALU.mult))
            score_free[0] = m
            yield
            m = DVE.chain(dve_side, [m],
                          lambda: V.tensor_reduce(wsum0[:, :], row(ra[:, :]), axis=AX, op=ALU.add),
                          lambda: V.tensor_scalar(wsum0[:, :], wsum0[:, :], EPS_W, None, ALU.add),
                          lambda: V.reciprocal(wsum0[:, :], wsum0[:, :]),
                          lambda: V.tensor_tensor(row(ra[:, :]), row(ra[:, :]), wsum0[:, :].unsqueeze(2).to_broadcast(by_tok), ALU.mult))
            yield
            m = DVE.put(dve_side, [m, coef_free[0]],
                        *[lambda n=n: V.tensor_scalar(coef[:, :, n], row(ra[:, :]), SCALE0, None, ALU.mult) for n in range(2)])
            yield
            yield from coef_to_columns(key, m)

        att1 = {"msg_free": [None] * 3}

        def setup1():
            over = [mark for _, mark in free_banks] + [coefT_ready[CHUNKS - 1], mix_ready[CHUNKS - 1]]
            raw1 = scores[:, :, :].rearrange("p a b -> p (a b)")[:, 0:5 * P + EXPERTS1]
            raw_ready = SP.put(att1_raw_in, over, lambda: nc.sync.dma_start(raw1, att1_w), by=16)
            load(att1_in, causal[:, :], att1_c)
            load(att1_in, f1[:, :], att1_f)
            att1["in"] = load(att1_in, b1[:, :], att1_b)
            att1["zero"] = POOL.put(pool_setup, over + [coef_free[0]],
                                    lambda: G.memset(near[:, :, 0:WINDOW], 0.0),
                                    lambda: G.memset(coef[:, :, :, :], 0.0))
            yield
            yield
            att1["w"] = split_small(w1, raw1, [raw_ready, *over])
            yield

        def w1_part(n):
            return (w1[:, 0, n * P:(n + 1) * P], w1[:, 1, n * P:(n + 1) * P])

        place = [(s, at, width) for s in range(SEQS) for at, width in KEYS]

        def attention1(key, c):
            xt, rows = columns_and_rows(key)
            b, ps, free = yield from take()
            mark = PE.put(pe_side, [xnT_ready[key], att1["w"], free], *mm3(ps[:, :], w1_part(0), xt))
            give(b, SCAL.put(act_side, [mark, att1["in"]], lambda ps=ps: A.activation(qT[:, :], ps[:, :], ACT.Identity, bias=b_q)))
            yield
            b, ps, free = yield from take()
            mark = PE.put(pe_side, [free], *mm3(ps[:, :], w1_part(1), xt))
            qk_ready = SCAL.put(act_side, [mark], lambda ps=ps: A.activation(kT[:, :], ps[:, :], ACT.Identity, bias=b_k))
            give(b, qk_ready)
            yield
            b, ps, free = yield from take()
            mark = PE.put(pe_side, [free], *[f for r in range(ROWS) for f in mm3(ps[:, r * P:(r + 1) * P], rows[r], w1_part(2))])
            v_ready = SCAL.put(act_side, [mark], lambda ps=ps: A.copy(v1[:, :], ps[:, :]))
            give(b, v_ready)
            yield
            masked = []
            for s in range(SEQS):
                b, ps, free = yield from take()
                mark = PE.put(pe_side, [qk_ready, free],
                              *[f for n, (at, width) in enumerate(KEYS) for f in
                                mm(ps[:, at:at + width], qT[:, s * SEQ + n * P:s * SEQ + (n + 1) * P], kT[:, s * SEQ:s * SEQ + width])])
                yield
                m = DVE.put(dve_side, [mark, att1["in"]],
                            lambda ps=ps, s=s: V.tensor_tensor(scores[:, s], ps[:, 0:KEYCOLS], causal[:, :], ALU.add))
                give(b, m)
                masked.append(m)
            b, ps, free = yield from take()
            mark = PE.put(pe_side, [free], *mm3(ps[:, :], w1_part(4), xt))
            near_in = SCAL.put(act_side, [mark, att1["zero"]], lambda ps=ps: A.copy(near[:, :, WINDOW:], seqs(ps[:, :])))
            give(b, near_in)
            m = DVE.put(dve_side, masked,
                        *[lambda r=r, s=s, at=at, wd=wd: V.max(best1[:, r], scores[:, s, at:at + wd]) for r, (s, at, wd) in enumerate(place)])
            yield
            scale = float(P) ** -0.5
            neg = DVE.put(dve_side, [m], lambda: V.tensor_scalar(top_neg[:, :], best1[:, :, 0], -scale, None, ALU.mult))
            for s in range(SEQS):
                m = DVE.put(dve_side, [m],
                            *[lambda r=r, s=s, at=at, wd=wd: V.match_replace(
                                out=rest[:, s, at:at + wd], in_to_replace=best1[:, r], in_values=scores[:, s, at:at + wd], imm_value=FAR)
                              for r, (q, at, wd) in enumerate(place) if q == s])
                yield (EXP if s else None)
            e_mark = SCAL.put(act_side, [m, neg],
                              *[lambda r=r, s=s, at=at, wd=wd, t=t: A.activation(
                                  t[:, s, at:at + wd], t[:, s, at:at + wd], ACT.Exp, bias=top_neg[:, r:r + 1], scale=scale)
                                for t in (scores, rest) for r, (s, at, wd) in enumerate(place)])
            b_self, ps_self, free = yield from take()
            self_half = PE.put(pe_side, [free], *mm3(ps_self[:, :], w1_part(3), xt))
            yield
            heard = None
            msg_free = att1["msg_free"]
            p_sum = e_mark
            for k in range(1, WINDOW + 1):
                slot = 0 if k == 1 else 1 + k % 2
                added = DVE.put(dve_side, [self_half, near_in, msg_free[slot]],
                                lambda k=k, slot=slot: V.tensor_tensor(
                                    seqs(msg[:, slot]), seqs(ps_self[:, :]), near[:, :, WINDOW - k:WINDOW - k + SEQ], ALU.add))
                act = SCAL.put(act_side, [added], lambda slot=slot: A.activation(msg[:, slot], msg[:, slot], ACT.Silu, bias=b_m1))
                if k > 1:
                    heard = POOL.put(pool_side, [act, heard, first_act], lambda slot=slot: G.tensor_tensor(msg[:, 0], msg[:, 0], msg[:, slot], ALU.add))
                    msg_free[slot] = heard
                else:
                    first_act = act
                r = k - 1
                s, at, wd = place[r]
                p_sum = DVE.put(dve_side, [e_mark], lambda r=r, s=s, at=at, wd=wd: V.scalar_tensor_tensor(
                    rest[:, s, at:at + wd], scores[:, s, at:at + wd], 1.0, rest[:, s, at:at + wd], ALU.mult, ALU.subtract,
                    accum_out=psum1[:, r:r + 1]))
                yield
            give(b_self, added)
            m = DVE.put(dve_side, [p_sum], lambda: V.reciprocal(psum1[:, :], psum1[:, :]))
            for s in range(SEQS):
                m2 = DVE.put(dve_side, [m],
                             *[lambda r=r, s=s, at=at, wd=wd: V.tensor_scalar(
                                 rest[:, s, at:at + wd], rest[:, s, at:at + wd], psum1[:, r:r + 1], None, ALU.mult)
                               for r, (q, at, wd) in enumerate(place) if q == s])
                yield
                b, ps, free = yield from take()
                mark = PE.put(pe_side, [m2, free],
                              *[lambda k=k, s=s, ps=ps: T.transpose(ps[:, k * P:(k + 1) * P], rest[:, s, k * P:(k + 1) * P], ident) for k in range(3)])
                pt = SCAL.put(act_side, [mark], lambda ps=ps, s=s: A.copy(scores[:, s], ps[:, 0:KEYCOLS]))
                give(b, pt)
            yield
            b, ps, free = yield from take()
            products = []
            for s in range(SEQS):
                v_a, v_b = (v1[:, r * P:(r + 1) * P] for r in (2 * s, 2 * s + 1))
                at = s * SEQ
                products += mm(ps[:, at:at + P], v_a, scores[:, s, 0:P])
                products += mm(ps[:, at + P:at + SEQ], v_a, scores[:, s, P:2 * P], stop=False)
                products += mm(ps[:, at + P:at + SEQ], v_b, scores[:, s, 2 * P:3 * P], start=False)
            mark = PE.put(pe_side, [pt, v_ready, free], *products)
            glob = SCAL.put(act_side, [mark, mix_free[0]], lambda ps=ps: A.activation(mix_b[:, :], ps[:, :], ACT.Identity, bias=b_v))
            give(b, glob)
            yield
            b, ps, free = yield from take()
            mark = PE.put(pe_side, [heard, free], *mm(ps[:, :], w_m2, msg[:, 0]))
            msg_free[0] = mark
            mix_ready[key] = SCAL.put(act_side, [mark, mix_free[0]], lambda ps=ps: A.activation(
                mix_a[:, :], ps[:, :], ACT.Identity, bias=b_m2, scale=1.0 / WINDOW))
            give(b, mix_ready[key])
            yield

        def routing1(key, c):
            yield from layer_norm(key, c, x1_ready[c])
            _, rows = columns_and_rows(key)
            by_e = [P, ROWS, EXPERTS1]
            b, ps, free = yield from take()
            mark = PE.put(pe_side, [xnT_ready[key], att1["w"], free],
                          *[f for r in range(ROWS) for f in
                            mm3(ps[:, r * EXPERTS1:(r + 1) * EXPERTS1], rows[r], (w1[:, 0, 5 * P:], w1[:, 1, 5 * P:]))])
            yield
            logits = ps[:, 0:ROWS * EXPERTS1].rearrange("p (r e) -> p r e", r=ROWS)
            m = DVE.chain(dve_side, [mark, att1["zero"]],
                          lambda: V.tensor_reduce(gsum[:, :], logits, axis=AX, op=ALU.max),
                          lambda: V.tensor_tensor(gate[:, :, :], logits, gsum[:, :].unsqueeze(2).to_broadcast(by_e), ALU.subtract))
            give(b, m)
            yield EXP
            m = SCAL.put(act_side, [m], lambda: A.activation(gate[:, :, :], gate[:, :, :], ACT.Exp))
            yield
            m = DVE.chain(dve_side, [m],
                          lambda: V.tensor_reduce(gsum[:, :], gate[:, :, :], axis=AX, op=ALU.add),
                          lambda: V.reciprocal(gsum[:, :], gsum[:, :]),
                          lambda: V.tensor_tensor(gate[:, :, :], gate[:, :, :], gsum[:, :].unsqueeze(2).to_broadcast(by_e), ALU.mult))
            yield
            m = yield from rank_among_8(gate[:, :, :], ROWS, ga[:, :], gb[:, :], gsel[:, :, :], [m, common_ready])
            yield
            m = DVE.chain(dve_side, [m],
                          lambda: V.tensor_scalar(gsel[:, :, :], gsel[:, :, :], TOP1 - 0.5, None, ALU.is_lt),
                          lambda: V.tensor_tensor(gate[:, :, :], gate[:, :, :], gsel[:, :, :], ALU.mult),
                          lambda: V.tensor_reduce(gsum[:, :], gate[:, :, :], axis=AX, op=ALU.add))
            yield
            m = DVE.chain(dve_side, [m],
                          lambda: V.reciprocal(gsum[:, :], gsum[:, :]),
                          lambda: V.tensor_tensor(gate[:, :, :], gate[:, :, :], gsum[:, :].unsqueeze(2).to_broadcast(by_e), ALU.mult))
            twice = [P, ROWS, EXPERTS1, 2]
            m = DVE.put(dve_side, [m, coef_free[0]],
                        *[lambda n=n: V.tensor_copy(coef[:, :, n, 0:2 * EXPERTS1].rearrange("p r (e t) -> p r e t", t=2),
                                                    gate[:, :, :].unsqueeze(3).to_broadcast(twice)) for n in range(2)])
            yield
            yield from coef_to_columns(key, m)

        x1_ready = [None] * CHUNKS

        def finish(layer, c, y_mark):
            b, ps, free = yield from take()
            mark = PE.put(pe_side, [y_mark, free, common_ready],
                          *[lambda r=r: T.transpose(ps[:, r * P:(r + 1) * P], swing[:, r * P:(r + 1) * P], ident) for r in range(ROWS)])
            swing_free[0] = mark
            yield
            mark = DVE.put(dve_side, [mark], lambda: V.tensor_tensor(
                xres[:, c], ps[:, :].rearrange("p (r d) -> p r d", r=ROWS), xres[:, c], ALU.add))
            give(b, mark)
            x1_ready[c] = mark
            if layer == 1:
                SP.put(stored, [mark], lambda: nc.sync.dma_start(out_rows[c], xres[:, c]), by=16)
            yield

        tiles = [(0, c, j) for c in range(CHUNKS) for j in range(TILES0)] + \
                [(1, c, j) for c in range(CHUNKS) for j in range(TILES1)]
        hist = []

        picked = {}

        def routed_pair(g):
            layer, c, j = tiles[g]
            if layer == 0:
                return j if j < TILES0 - 1 else None
            return j // 2 if j % 2 == 0 else None

        def pick_experts(g):
            pair = routed_pair(g)
            if pair is None:
                return
            picked[g] = DVE.put(dve_pick, [common_ready, pick_free[pair % 2]], lambda: V.tensor_copy(
                pick_pair[:, pair % 2], pick[:, 2 * pair:2 * pair + 2].unsqueeze(2).to_broadcast([P, 2, 64])))

        def first_products(g):
            layer, c, j = tiles[g]
            key = c + layer * CHUNKS
            buf = key % 2
            xt = (xnT[:, buf, 0], xnT[:, buf, 1])
            w_gate, w_up, _ = tile_weights(j)
            m = {}
            two = hist[g - 2] if g >= 2 else {}
            split = list(w_split[j + layer * TILES0]) if c == 0 else []
            m["gate"] = PE.put(pe_gate, [xnT_ready[key], two.get("silu"), *split], *mm3(ps_gate[g % 2][:, :], w_gate, xt))
            m["up"] = PE.put(pe_up, [two.get("h1")], *mm3(ps_up[g % 2][:, :], w_up, xt))
            routed = not (layer == 0 and j == TILES0 - 1)
            pair = routed_pair(g)
            if pair is not None:
                sel = pick_pair[:, pair % 2].rearrange("p a b -> p (a b)")
                m["coef"] = PE.put(pe_coef, [coefT_ready[key], picked[g], coef_read[0]],
                                   *mm(ps_coef[:, :], sel, coefT[:, buf]))
                coefT_free[buf] = pick_free[pair % 2] = m["coef"]
            else:
                m["coef"] = hist[g - 1]["coef"] if routed else None
            xnT_free[buf] = m["up"]
            hist.append(m)

        coef_read = [None]
        pick_free = [None, None]

        def times_coef(g):
            m = hist[g]
            s = g % 3
            if m["coef"] is None:
                m["h"] = m["h1"]
                return
            m["h"] = DVE.put(dve_coef, [m["h1"], m["coef"]],
                             lambda: V.tensor_tensor(silu_h[:, s], ps_coef[:, :], silu_h[:, s], ALU.mult))
            coef_read[0] = m["h"]

        def silu_and_up(g):
            m = hist[g]
            s = g % 3
            lo3 = hist[g - 3]["lo"] if g >= 3 else w0_ready
            m["silu"] = SCAL.put(act_silu, [m["gate"], lo3], lambda: A.activation(silu_h[:, s], ps_gate[g % 2][:, :], ACT.Silu))
            m["h1"] = DVE.put(dve_up, [m["silu"], m["up"]],
                              lambda: V.tensor_tensor(silu_h[:, s], ps_up[g % 2][:, :], silu_h[:, s], ALU.mult))

        def split_h(g):
            m = hist[g]
            s = g % 3
            down3 = hist[g - 3].get("down") if g >= 3 else None
            m["hi"] = SCAL.put(act_hi, [m["h"], down3], lambda: A.copy(h_hi[:, s], silu_h[:, s]))
            m["lo"] = POOL.put(pool_lo, [m["hi"], down3], lambda: G.tensor_tensor(h_lo[:, s], silu_h[:, s], f32(h_hi[:, s]), ALU.subtract))

        y_free = [None]

        def last_products(g):
            layer, c, j = tiles[g]
            m = hist[g]
            s = g % 3
            key = c + layer * CHUNKS
            _, _, w_down = tile_weights(j)
            last = j == (TILES1 if layer else TILES0) - 1
            if last:
                mixed = [(w_out[:, :], mix_a)] if layer == 0 else [(w_ol, mix_a), (w_og, mix_b)]
                mix_free[0] = PE.put(pe_mix, [mix_ready[key], att0_ready if layer == 0 else att1["in"]],
                                     *[f for w, mix in mixed for f in mm(ps_y[:, :], w, mix[:, :], start=False, stop=False)])
            m["down"] = PE.put(pe_down, [m["hi"], m["lo"], y_free[0]],
                               *mm3(ps_y[:, :], w_down, (h_hi[:, s], h_lo[:, s]), start=j == 0, stop=last))
            if last:
                bias = b_o if layer else None
                copy = (lambda: A.activation(swing[:, :], ps_y[:, :], ACT.Identity, bias=bias)) if layer else \
                    (lambda: A.copy(swing[:, :], ps_y[:, :]))
                y_free[0] = SCAL.put(act_y, [m["down"], swing_free[0]], copy)
                swing_free[0] = y_free[0]
                return finish(layer, c, y_free[0])
            return None

        def drain(steps):
            for _ in steps:
                pass

        ATT_STEPS = [["attention", "route"], ["attention", "route", "attention", "route"]]
        PATIENCE = 8
        AHEAD = 3
        for j in range(AHEAD):
            split_tile(0, j)
        drain(routing0(0, 0))

        class Side:

            def __init__(self):
                self.pieces, self.held, self.patience = [], [], 0

            def add(self, name, steps):
                self.pieces.append((name, steps))

            def step(self, name):
                steps = dict(self.pieces).get(name)
                if steps is None:
                    return
                if name in self.held:
                    self.patience -= 1
                else:
                    said = next(steps, "end")
                    if said == "end":
                        self.pieces.remove((name, steps))
                    elif said == EXP:
                        self.held.append(name)
                        self.patience = PATIENCE
                if self.held and (self.patience == 0 or len(self.held) == len(self.pieces)):
                    going, self.held = self.held, []
                    for n in going:
                        self.step(n)

            def end(self):
                while self.pieces:
                    for n, _ in list(self.pieces):
                        self.step(n)

        side = Side()
        pick_experts(0)
        for g, (layer, c, j) in enumerate(tiles):
            done = None
            n_tiles = TILES1 if layer else TILES0
            if j == 0:
                side.add("attention", attention1(CHUNKS + c, c) if layer else attention0(c, c))
            if g >= LAG:
                done = last_products(g - LAG)
            if g >= 1:
                times_coef(g - 1)
            first_products(g)
            silu_and_up(g)
            if g + 1 < len(tiles):
                pick_experts(g + 1)
            if g >= 1:
                split_h(g - 1)
            if layer == 0 and c == 0 and j + AHEAD < TILES0:
                split_tile(0, j + AHEAD)
            if layer == 0 and c == CHUNKS - 1:
                k = j - LAG - 1
                if 0 <= k < TILES1:
                    split_tile(1, k, free=[hist[g - LAG - 1]["down"]])
            if layer == 0 and c == 0 and j == TILES0 - 1:
                for cc in range(3, CHUNKS):
                    x_ready[cc] = load(x_in[cc], xres[:, cc], x_rows[cc])
            if done is not None:
                closing = done
            if j == LAG - 1:
                def route(layer=layer, c=c, closing=closing if g >= LAG else iter(())):
                    yield from closing
                    if layer == 0 and c < CHUNKS - 1:
                        yield from routing0(c + 1, c + 1)
                    elif layer == 0:
                        while CHUNKS - 1 not in mix_ready:
                            yield
                        yield from setup1()
                        yield from routing1(CHUNKS, 0)
                    elif c < CHUNKS - 1:
                        yield from routing1(CHUNKS + c + 1, c + 1)
                side.add("route", route())
            for name in ATT_STEPS[layer]:
                side.step(name)
            if j == n_tiles - 1:
                side.end()
        n = len(tiles)
        for k in range(3):
            if k == 0:
                times_coef(n - 1)
                split_h(n - 1)
            done = last_products(n - LAG + k)
        drain(done)
        SP_last = (stored, stored.n)

        block = ctx.enter_context(nc.Block())

        @block.sync
        def _(eng):
            SP.run(eng)
            eng.wait_ge(SP_last[0].sem, SP_last[1])

        @block.tensor
        def _(eng):
            PE.run(eng)

        @block.vector
        def _(eng):
            DVE.run(eng)

        @block.scalar
        def _(eng):
            SCAL.run(eng)

        @block.gpsimd
        def _(eng):
            POOL.run(eng)


def shape_constants():
    ident = np.eye(P, dtype=np.float32)
    pick = (np.arange(P)[:, None] % 64 == np.arange(64)[None, :]).astype(np.float32)
    earlier = np.broadcast_to((np.arange(8)[None, :] < np.arange(8)[:, None]).astype(np.float32).reshape(1, 64), (P, 64))
    common = np.concatenate([ident, pick, earlier], 1)
    head = np.arange(P) // HEAD
    same_head = (head[:, None] == head[None, :]).astype(np.float32)
    inv_freq = (np.float32(1.0) / np.float32(ROPE_BASE) ** (np.arange(0, HEAD, 2, dtype=np.float32) / np.float32(HEAD))).astype(np.float32)
    freqs = np.arange(SEQ, dtype=np.float32)[:, None] * inv_freq[None, :]
    angle = np.tile(np.concatenate([freqs, freqs], 1), (1, HEADS))
    cos, sin = np.cos(angle), np.sin(angle)
    sign = np.where(np.arange(P) % HEAD < HEAD // 2, -1.0, 1.0).astype(np.float32)
    sin = sin * sign[None, :]
    scale = np.float32(HEAD ** -0.5)
    by_row = lambda t: t.reshape(2, P, P).transpose(1, 0, 2).reshape(P, SEQ)
    att0 = np.concatenate([same_head, cos.T * scale, sin.T * scale, by_row(cos), by_row(sin)], 1)
    tri = np.where(np.arange(P)[None, :] > np.arange(P)[:, None], FAR, 0.0)
    att1 = np.concatenate([tri, np.zeros((P, P)), tri], 1)
    return tuple(np.ascontiguousarray(t.astype(np.float32)) for t in (common, att0, att1))


def kernel(**inputs):
    import concourse.bacc as bacc
    from concourse.bass_utils import run_bass_kernel_spmd

    a = {k: np.asarray(v) for k, v in inputs.items()}
    cat = np.concatenate
    common_c, att0_c, att1_c = shape_constants()

    pairs = EXPERTS0 * FF0 // P

    def paired(w):
        return w.reshape(pairs, 2, P, FF0).transpose(0, 2, 1, 3).reshape(pairs, P, P)

    tiles0 = cat([paired(a["L0_ffn_Wg"]), paired(a["L0_ffn_Wu"]), a["L0_ffn_Wd"].reshape(pairs, P, P)], 2)
    shared = cat([a["L0_ffn_SWg"], a["L0_ffn_SWu"], a["L0_ffn_SWd"]], 1)[None]

    def halves(w):
        return w.reshape(TILES1, P, P).transpose(0, 2, 1)

    down1 = a["L1_ffn_w2"].reshape(EXPERTS1, P, 2, P).transpose(0, 2, 3, 1).reshape(TILES1, P, P)
    tiles1 = cat([halves(a["L1_ffn_w1"]), halves(a["L1_ffn_w3"]), down1], 2)
    ffn_w = cat([tiles0, shared, tiles1], 0)
    wq, wk, wv = np.split(a["L0_attn_W_qkv"], 3, axis=1)
    swap = (np.arange(P) // HEAD) * HEAD + (np.arange(P) % HEAD + HEAD // 2) % HEAD
    att0_w = cat([wq, wq[:, swap], wk, wk[:, swap], wv, a["L0_ffn_router_w"].T], 1)
    wm1, wo = a["L1_attn_Wm1"], a["L1_attn_Wo"]
    att1_w = cat([a["L1_attn_Wq"], a["L1_attn_Wk"], a["L1_attn_Wv"], wm1[:P], wm1[P:], a["L1_ffn_gate_w"].T], 1)
    att1_f = cat([a["L1_attn_Wm2"], wo[:P], wo[P:]], 1)
    att1_b = np.stack([a[f"L1_attn_{n}"] for n in ("bq", "bk", "bv", "bm1", "bm2", "bo")], 1)
    arrays = {
        "x": a["L0_attn_x"].reshape(TOKENS, P), "ffn_w": ffn_w, "att0_w": att0_w, "att0_f": a["L0_attn_W_out"],
        "att0_c": att0_c, "e_bias": a["L0_ffn_e_bias"], "att1_w": att1_w, "att1_f": att1_f, "att1_b": att1_b,
        "att1_c": att1_c, "common_c": common_c,
    }
    arrays = {k: np.ascontiguousarray(v) for k, v in arrays.items()}
    nc = bacc.Bacc("TRN2", target_bir_lowering=False, num_devices=1)
    args = [nc.dram_tensor(f"in_{k}", v.shape, mybir.dt.from_np(v.dtype), kind="ExternalInput").ap() for k, v in arrays.items()]
    out = nc.dram_tensor("out", (TOKENS, P), FP32, kind="ExternalOutput").ap()
    build_program(nc, *args, out)
    r = run_bass_kernel_spmd(nc, [{f"in_{k}": v for k, v in arrays.items()}], core_ids=[0])
    return r.results[0]["out"].reshape(a["L0_attn_x"].shape)
```

```python
from contextlib import ExitStack

import concourse.bass as bass
import numpy as np
from concourse import mybir

FP32 = mybir.dt.float32
FP32R = mybir.dt.float32r
ALU = mybir.AluOpType
ACT = mybir.ActivationFunctionType
AX = mybir.AxisListType.X

P = 128
SEQ = 256
TOKENS = 32 * SEQ
CHUNK = 512
ROWS = CHUNK // P
SEQS = CHUNK // SEQ
CHUNKS = TOKENS // CHUNK
HEADS, HEAD = 16, 8
ROPE_BASE = 500000.0
EXPERTS0, FF0, GROUPS0, TOP_GROUPS0, TOP0, SCALE0 = 64, 64, 8, 4, 8, 2.5
EXPERTS1, FF1, TOP1 = 8, 256, 2
WINDOW, TOP_KEYS = 4, 8
TILES0 = EXPERTS0 * FF0 // P + 1
TILES1 = EXPERTS1 * FF1 // P
FAR = -1.0e30
EPS_LN, EPS_DEN, EPS_W = 1e-5, 1e-6, 1e-20
KEYS = [(0, P), (P, SEQ)]
KEYCOLS = P + SEQ
STAGES_W = 4
LAG = 3
EXP = "exp"


class Stage:

    def __init__(self, sem):
        self.sem, self.n = sem, 0

    def done(self, by=1):
        self.n += by
        return (self, self.n)


class Line:

    def __init__(self):
        self.items, self.seen = [], {}

    def put(self, stage, waits, *instructions, by=1):
        need = []
        for mark in waits:
            if mark is not None and self.seen.get(mark[0], 0) < mark[1]:
                self.seen[mark[0]] = mark[1]
                need.append(mark)
        mark = stage.done(by)
        self.items.append((need, instructions, stage, by))
        return mark

    def chain(self, stage, waits, *instructions):
        mark = None
        for n, one in enumerate(instructions):
            mark = self.put(stage, waits if n == 0 else [mark], one)
        return mark

    def run(self, engine):
        for need, instructions, stage, by in self.items:
            for sem_stage, value in need:
                engine.wait_ge(sem_stage.sem, value)
            for one in instructions:
                last = one()
            last.then_inc(stage.sem, by)


def build_program(nc, x, ffn_w, att0_w, att0_f, att0_c, e_bias, att1_w, att1_f, att1_b, att1_c, common_c, out):
    ctx = ExitStack()
    with ctx:
        def sb(name, shape, dtype=FP32, within=ctx):
            return within.enter_context(nc.sbuf_tensor(name, [P] + list(shape), dtype))

        def stage(name):
            return Stage(ctx.enter_context(nc.semaphore(name)))

        xres = sb("xres", [CHUNKS, ROWS, P])
        w_gu = sb("w_gu", [TILES0, 2, 2, P], FP32R)
        w_dn = sb("w_dn", [TILES0, 2, P], FP32R)
        w_raw = sb("w_raw", [STAGES_W, 3, P])
        xnT = sb("xnT", [2, 2, CHUNK], FP32R)
        coefT = sb("coefT", [2, CHUNK], FP32R)
        coef = sb("coef", [ROWS, 2, 64])
        silu_h = sb("silu_h", [3, CHUNK])
        h_hi = sb("h_hi", [3, CHUNK], FP32R)
        h_lo = sb("h_lo", [3, CHUNK], FP32R)
        yT = sb("yT", [CHUNK])
        norm_rows = sb("norm_rows", [CHUNK])
        above, equal = norm_rows[:, 0:ROWS * 64], norm_rows[:, ROWS * 64:]
        mix_a = sb("mix_a", [CHUNK])
        common = sb("common", [P + 64 + 64])
        ident, pick, earlier = common[:, 0:P], common[:, P:P + 64], common[:, P + 64:P + 128]
        w_out = sb("w_out", [P])
        pick_pair = sb("pick_pair", [2, 2, 64], FP32R)
        stats = sb("stats", [ROWS, 6])
        mean_var = sb("mean_var", [ROWS, 2])
        rstd = sb("rstd", [ROWS])
        minus_half = sb("minus_half", [ROWS])

        in0 = ExitStack()
        c0 = sb("att0_const", [P + 4 * SEQ], within=in0)
        same_head = c0[:, 0:P]
        cosq, sinq, cosk, sink = (c0[:, P + n * SEQ:P + (n + 1) * SEQ] for n in range(4))
        w0 = sb("w0", [2, 4 * P + EXPERTS0], FP32R, within=in0)
        bias0 = sb("bias0", [EXPERTS0], within=in0)
        kf = sb("kf", [CHUNK], within=in0)
        qf = sb("qf", [CHUNK], within=in0)
        tmp0 = sb("tmp0", [CHUNK], within=in0)
        k_low = sb("k_low", [CHUNK], within=in0)
        v0 = sb("v0", [ROWS, P + 1], within=in0)
        kv = sb("kv", [SEQS, 2, P], within=in0)
        score0 = sb("score0", [ROWS * EXPERTS0], within=in0)
        sfc = sb("sfc", [ROWS * EXPERTS0], within=in0)
        hi4 = sb("hi4", [ROWS * GROUPS0, 4], within=in0)
        lo4 = sb("lo4", [ROWS * GROUPS0, 4], within=in0)
        hi2 = sb("hi2", [ROWS * GROUPS0, 2], within=in0)
        mi2 = sb("mi2", [ROWS * GROUPS0, 2], within=in0)
        lo2 = sb("lo2", [ROWS * GROUPS0, 2], within=in0)
        g_a = sb("g_a", [ROWS * GROUPS0], within=in0)
        g_b = sb("g_b", [ROWS * GROUPS0], within=in0)
        best0 = sb("best0", [ROWS, 8], within=in0)
        wsum0 = sb("wsum0", [ROWS], within=in0)
        in0.close()

        in1 = ExitStack()
        causal = sb("causal", [KEYCOLS], within=in1)
        w1 = sb("w1", [2, 5 * P + EXPERTS1], FP32R, within=in1)
        f1 = sb("f1", [3 * P], within=in1)
        w_m2T, w_ol, w_og = (f1[:, n * P:(n + 1) * P] for n in range(3))
        w_local = w_m2T
        b1 = sb("b1", [6], within=in1)
        b_q, b_k, b_v, b_m1, b_m2, b_o = (b1[:, n:n + 1] for n in range(6))
        qT = sb("qT", [CHUNK], within=in1)
        kT = sb("kT", [CHUNK], within=in1)
        v1 = sb("v1", [CHUNK], within=in1)
        scores = sb("scores", [SEQS, KEYCOLS], within=in1)
        rest = sb("rest", [SEQS, KEYCOLS], within=in1)
        near = sb("near", [SEQS, WINDOW + SEQ], within=in1)
        msg = sb("msg", [3, CHUNK], within=in1)
        best1 = sb("best1", [ROWS, 8], within=in1)
        top_neg = sb("top_neg", [ROWS], within=in1)
        psum1 = sb("psum1", [ROWS], within=in1)
        gate = sb("gate", [ROWS, EXPERTS1], within=in1)
        gsel = sb("gsel", [ROWS, EXPERTS1], within=in1)
        gsum = sb("gsum", [ROWS], within=in1)
        in1.close()

        def bank(name):
            return ctx.enter_context(nc.psum_tensor(name, [P, CHUNK], FP32))

        ps_gate = [bank("ps_gate0"), bank("ps_gate1")]
        ps_up = [bank("ps_up0"), bank("ps_up1")]
        ps_coef = bank("ps_coef")
        ps_y = bank("ps_y")
        ps_side = [bank("ps_side0"), bank("ps_side1")]

        x_in = [stage(f"x_in{c}") for c in range(CHUNKS)]
        w_in = [stage(f"w_in{n}") for n in range(STAGES_W)]
        const_in = stage("const_in")
        att0_in = stage("att0_in")
        att1_in = stage("att1_in")
        att1_raw_in = stage("att1_raw_in")
        stored = stage("stored")
        pe_gate, pe_up, pe_coef, pe_down, pe_mix = (stage(n) for n in ("pe_gate", "pe_up", "pe_coef", "pe_down", "pe_mix"))
        act_silu, act_hi, act_whi, act_y = (stage(n) for n in ("act_silu", "act_hi", "act_whi", "act_y"))
        dve_up, dve_coef, dve_wlo = (stage(n) for n in ("dve_up", "dve_coef", "dve_wlo"))
        pool_lo, pool_pick = stage("pool_lo"), stage("pool_pick")
        pe_side, act_side, dve_side, pool_side = (stage(n) for n in ("pe_side", "act_side", "dve_side", "pool_side"))
        dve_setup, pool_setup, act_setup = stage("dve_setup"), stage("pool_setup"), stage("act_setup")

        PE, SCAL, DVE, POOL, SP = (Line() for _ in range(5))
        T, A, V, G = nc.tensor, nc.scalar, nc.vector, nc.gpsimd

        def f32(ap):
            return ap.bitcast(FP32)

        def mm3(dst, w, m, start=True, stop=True):
            return [lambda: T.matmul(dst, w[0], m[0], start=start, stop=False),
                    lambda: T.matmul(dst, w[1], m[0], start=False, stop=False),
                    lambda: T.matmul(dst, w[0], m[1], start=False, stop=stop)]

        def mm(dst, w, m, start=True, stop=True):
            return [lambda: T.matmul(dst, w, m, start=start, stop=stop)]

        def router_products(ps, r, experts, row, w):
            at = r * 2 * experts
            return [lambda: T.matmul(ps[:, at:at + 2 * experts], row[0], w, start=True, stop=False),
                    lambda: T.matmul(ps[:, at:at + experts], row[1], w[:, 0], start=False, stop=True)]

        def load(stg, dst, src):
            return SP.put(stg, [], lambda: nc.sync.dma_start(dst, src), by=16)

        x_rows = x.rearrange("(c r p) d -> c p r d", r=ROWS, p=P)
        out_rows = out.rearrange("(c r p) d -> c p r d", r=ROWS, p=P)
        raw0 = silu_h[:, :, :].rearrange("p a b -> p (a b)")[:, 0:4 * P + EXPERTS0]
        x_ready = [None] * CHUNKS
        x_ready[0] = load(x_in[0], xres[:, 0], x_rows[0])
        common_ready = load(const_in, common[:, :], common_c)
        load(att0_in, raw0, att0_w)
        load(att0_in, c0[:, :], att0_c)
        load(att0_in, w_out[:, :], att0_f)
        att0_ready = load(att0_in, bias0[:, :], e_bias.partition_broadcast(P))

        w_split = [None] * (TILES0 + TILES1)
        w_loaded = [None] * (TILES0 + TILES1)

        def load_tile(n):
            waits = list(w_split[n - STAGES_W]) if n >= STAGES_W else []
            w_loaded[n] = SP.put(w_in[n % STAGES_W], waits,
                                 lambda: nc.sync.dma_start(w_raw[:, n % STAGES_W], ffn_w[n].rearrange("p (k d) -> p k d", k=3)), by=16)

        for n in range(STAGES_W):
            load_tile(n)
        for c in range(1, min(3, CHUNKS)):
            x_ready[c] = load(x_in[c], xres[:, c], x_rows[c])

        def tile_weights(j):
            gu, dn = w_gu[:, j], w_dn[:, j]
            return (gu[:, 0, 0], gu[:, 0, 1]), (gu[:, 1, 0], gu[:, 1, 1]), (dn[:, 0], dn[:, 1])

        def split_tile(layer, j, free=()):
            n = j + layer * TILES0
            raw = w_raw[:, n % STAGES_W]
            gu, dn = w_gu[:, j], w_dn[:, j]
            hi = SCAL.put(act_whi, [w_loaded[n], *free],
                          lambda: A.copy(gu[:, :, 0], raw[:, 0:2]),
                          lambda: A.copy(dn[:, 0], raw[:, 2]))
            lo = DVE.put(dve_wlo, [hi],
                         lambda: V.tensor_tensor(gu[:, :, 1], raw[:, 0:2], f32(gu[:, :, 0]), ALU.subtract),
                         lambda: V.tensor_tensor(dn[:, 1], raw[:, 2], f32(dn[:, 0]), ALU.subtract))
            w_split[n] = (hi, lo)
            if n + STAGES_W < TILES0 + TILES1:
                load_tile(n + STAGES_W)

        pow_ready = DVE.put(dve_setup, [], lambda: V.memset(minus_half[:, :], -0.5))
        ones_ready = DVE.put(dve_setup, [], lambda: V.memset(v0[:, :, P:], 1.0))

        def split_small(dst, raw, waits):
            hi = SCAL.put(act_setup, waits, lambda: A.copy(dst[:, 0], raw))
            return DVE.put(dve_setup, [hi], lambda: V.tensor_tensor(dst[:, 1], raw, f32(dst[:, 0]), ALU.subtract))


        turn = [0]
        free_banks = [(0, None, -1), (1, None, -1)]

        def take():
            while not free_banks or free_banks[0][2] == turn[0]:
                yield
            n, mark, _ = free_banks.pop(0)
            return n, ps_side[n], mark

        def settle():
            now = turn[0]
            while turn[0] == now:
                yield

        def give(n, mark):
            free_banks.append((n, mark, turn[0]))

        xnT_free = [None, None]
        coefT_free = [None, None]
        yT_free = [None]
        xnT_ready, coefT_ready, mix_ready, values_ready = {}, {}, {}, {}
        joined = set()
        mix_free = [None]
        score_free = [None]
        coef_free = [None]

        def layer_norm(key, c, x_mark):
            buf = key % 2
            mark = DVE.put(dve_side, [x_mark],
                           *[lambda r=r: V.bn_stats(stats[:, r], xres[:, c, r]) for r in range(ROWS)])
            mark = DVE.put(dve_side, [mark],
                           *[lambda r=r: V.bn_aggr(mean_var[:, r], stats[:, r]) for r in range(ROWS)])
            mark = DVE.put(dve_side, [mark], lambda: V.tensor_scalar(rstd[:, :], mean_var[:, :, 1], EPS_LN, None, ALU.add))
            mark = POOL.put(pool_side, [mark, pow_ready],
                            lambda: G.tensor_tensor(rstd[:, :], rstd[:, :], minus_half[:, :], ALU.pow))
            yield 2
            mark = DVE.put(dve_side, [mark],
                           *[lambda r=r: V.tensor_scalar(norm_rows[:, r * P:(r + 1) * P], xres[:, c, r], mean_var[:, r, 0:1],
                                                         rstd[:, r:r + 1], ALU.subtract, ALU.mult) for r in range(ROWS)])
            yield 1.7
            b, ps, free = yield from take()
            mark = PE.put(pe_side, [mark, free, common_ready],
                          *[lambda r=r: T.transpose(ps[:, r * P:(r + 1) * P], norm_rows[:, r * P:(r + 1) * P], ident)
                            for r in range(ROWS)])
            hi = SCAL.put(act_side, [mark, xnT_free[buf]], lambda: A.copy(xnT[:, buf, 0], ps[:, :]))
            yield
            lo = DVE.put(dve_side, [hi], lambda: V.tensor_tensor(xnT[:, buf, 1], ps[:, :], f32(xnT[:, buf, 0]), ALU.subtract))
            give(b, lo)
            xnT_ready[key] = lo
            yield 1

        def rank_among_8(values, rows, count, waits):
            shape = [P, rows, 8, 8]
            mine = values.unsqueeze(3).to_broadcast(shape)
            other = values.unsqueeze(2).to_broadcast(shape)
            first = earlier.rearrange("p (g h) -> p g h", g=8).unsqueeze(1).to_broadcast(shape)
            ab = above.rearrange("p (r g h) -> p r g h", g=8, h=8)
            eq = equal.rearrange("p (r g h) -> p r g h", g=8, h=8)
            m = DVE.put(dve_side, waits, lambda: V.tensor_tensor(ab, other, mine, ALU.is_gt),
                        lambda: V.tensor_tensor(eq, other, mine, ALU.is_equal))
            yield 1.2
            m = DVE.chain(dve_side, [m],
                          lambda: V.tensor_tensor(eq, eq, first, ALU.mult),
                          lambda: V.tensor_tensor(above, above, equal, ALU.add))
            yield 1.2
            return DVE.chain(dve_side, [m],
                             lambda: V.tensor_reduce(count, ab, axis=AX, op=ALU.add))

        def coef_to_columns(key, mark):
            buf = key % 2
            b, ps, free = yield from take()
            flat = coef[:, :, :, :].rearrange("p r a e -> p r (a e)")
            mark = PE.put(pe_side, [mark, free],
                          *[lambda r=r: T.transpose(ps[:, r * P:(r + 1) * P], flat[:, r], ident) for r in range(ROWS)])
            coef_free[0] = mark
            hi = SCAL.put(act_side, [mark, coefT_free[buf]], lambda: A.copy(coefT[:, buf], ps[:, :]))
            yield
            lo = DVE.put(dve_side, [hi], lambda: V.tensor_tensor(coefT[64:P, buf], ps[64:P, :], f32(coefT[64:P, buf]), ALU.subtract))
            give(b, lo)
            coefT_ready[key] = lo
            yield 1

        def columns_and_rows(key):
            buf = key % 2
            whole = (xnT[:, buf, 0], xnT[:, buf, 1])
            return whole, [(whole[0][:, r * P:(r + 1) * P], whole[1][:, r * P:(r + 1) * P]) for r in range(ROWS)]

        def seqs(ap):
            return ap.rearrange("p (s t) -> p s t", s=SEQS)

        def attention0(key, c):
            xt, rows = columns_and_rows(key)

            def w(lo, hi):
                return (w0[:, 0, lo:hi], w0[:, 1, lo:hi])

            for r in range(ROWS):
                b, ps, free = yield from take()
                mark = PE.put(pe_side, [xnT_ready[key], w0_ready, free, mix_free[0]], *mm3(ps[:, 0:2 * P], rows[r], w(2 * P, 4 * P)))
                yield (0.7 if r else 0)
                half = (r % 2) * P
                DVE.put(dve_side, [mark],
                        lambda ps=ps, r=r, half=half: V.tensor_tensor(kf[:, r * P:(r + 1) * P], ps[:, 0:P], cosk[:, half:half + P], ALU.mult))
                k_halves, sin_halves, out_halves = (ap.rearrange("p (h t d) -> p h t d", h=HEADS, t=2) for ap in (
                    ps[:, 0:P], sink[:, half:half + P], tmp0[:, r * P:(r + 1) * P]))
                k_parts = DVE.put(dve_side, [mark], *[
                    lambda t=t, k=k_halves, sin=sin_halves, o=out_halves: V.tensor_tensor(o[:, :, t], k[:, :, 1 - t], sin[:, :, t], ALU.mult)
                    for t in range(2)])
                v_ready = SCAL.put(act_side, [k_parts], lambda ps=ps, r=r: A.copy(v0[:, r, 0:P], ps[:, P:2 * P]))
                give(b, v_ready)
            k_rope = POOL.put(pool_side, [k_parts], lambda: G.tensor_tensor(kf[:, :], kf[:, :], tmp0[:, :], ALU.add))
            yield 0.7
            by_seq = [P, SEQS, SEQ]
            b, ps, free = yield from take()
            mark = PE.put(pe_side, [free], *mm3(ps[:, :], w(0, P), xt))
            yield
            mark = DVE.put(dve_side, [mark], lambda ps=ps: V.tensor_tensor(
                seqs(qf[:, :]), seqs(ps[:, :]), cosq.unsqueeze(1).to_broadcast(by_seq), ALU.mult))
            give(b, mark)
            b, ps, free = yield from take()
            mark = PE.put(pe_side, [free], *mm3(ps[:, :], w(P, 2 * P), xt))
            k_min = POOL.put(pool_side, [k_rope], lambda: G.tensor_scalar(k_low[:, :], kf[:, :], 0.0, None, ALU.min))
            yield 1
            mark = DVE.put(dve_side, [mark, k_rope], lambda ps=ps: V.tensor_tensor(
                seqs(tmp0[:, :]), seqs(ps[:, :]), sinq.unsqueeze(1).to_broadcast(by_seq), ALU.mult))
            give(b, mark)
            q_rope = POOL.put(pool_side, [mark], lambda: G.tensor_tensor(qf[:, :], qf[:, :], tmp0[:, :], ALU.add))
            yield 1
            q_min = POOL.put(pool_side, [q_rope], lambda: G.tensor_scalar(tmp0[:, :], qf[:, :], 0.0, None, ALU.min))
            yield
            yield EXP
            k_exp = SCAL.put(act_side, [k_min], lambda: A.activation(k_low[:, :], k_low[:, :], ACT.Exp))
            q_exp = SCAL.put(act_side, [q_min], lambda: A.activation(tmp0[:, :], tmp0[:, :], ACT.Exp))
            yield
            yield
            kf_ready = DVE.put(dve_side, [k_exp], lambda: V.scalar_tensor_tensor(kf[:, :], kf[:, :], 0.0, k_low[:, :], ALU.max, ALU.add))
            yield 1
            q_relu = SCAL.put(act_side, [q_exp], lambda: A.activation(qf[:, :], qf[:, :], ACT.Relu))
            qf_ready = POOL.put(pool_side, [q_relu], lambda: G.tensor_tensor(qf[:, :], qf[:, :], tmp0[:, :], ALU.add))
            yield
            b, ps, free = yield from take()
            products = []
            for s in range(SEQS):
                for r in (2 * s, 2 * s + 1):
                    products += mm(ps[:, s * (P + 1):(s + 1) * (P + 1)], kf[:, r * P:(r + 1) * P], v0[:, r], start=r == 2 * s, stop=r == 2 * s + 1)
            by_key = ps[:, 0:SEQS * (P + 1)].rearrange("p (s d) -> p s d", s=SEQS)
            mark = PE.put(pe_side, [kf_ready, v_ready, ones_ready, free], *products)
            yield
            kv_ready = DVE.put(dve_side, [mark],
                               lambda by_key=by_key: V.tensor_tensor(
                                   kv[:, :, 0], by_key[:, :, 0:P], same_head.unsqueeze(1).to_broadcast([P, SEQS, P]), ALU.mult),
                               *[lambda by_key=by_key, s=s: V.tensor_scalar(kv[:, s, 1], same_head, by_key[:, s, P:], None, ALU.mult)
                                 for s in range(SEQS)])
            give(b, kv_ready)
            yield 1.2

            def against_q(n, ps):
                return [f for s in range(SEQS) for f in mm(ps[:, s * SEQ:(s + 1) * SEQ], kv[:, s, n], qf[:, s * SEQ:(s + 1) * SEQ])]

            b, ps, free = yield from take()
            mark = PE.put(pe_side, [kv_ready, qf_ready, free], *against_q(1, ps))
            yield
            mark = DVE.put(dve_side, [mark], lambda ps=ps: V.tensor_scalar(tmp0[:, :], ps[:, :], EPS_DEN, None, ALU.max))
            give(b, mark)
            b, ps, free = yield from take()
            numerator = PE.put(pe_side, [free], *against_q(0, ps))
            yield 1
            inverse = []
            for r in range(ROWS):
                inverse.append(DVE.put(dve_side, [mark], lambda r=r: V.reciprocal(tmp0[:, r * P:(r + 1) * P], tmp0[:, r * P:(r + 1) * P])))
                yield 1.45
            mark = DVE.put(dve_side, [numerator, *inverse], lambda ps=ps: V.tensor_tensor(mix_a[:, :], ps[:, :], tmp0[:, :], ALU.mult))
            give(b, mark)
            mix_ready[key] = mark
            yield 1

        def routing0(key, c):
            yield from layer_norm(key, c, x_ready[c])
            _, rows = columns_and_rows(key)
            b, ps, free = yield from take()
            mark = PE.put(pe_side, [xnT_ready[key], w0_ready, free],
                          *[f for r in range(ROWS) for f in
                            mm3(ps[:, r * EXPERTS0:(r + 1) * EXPERTS0], rows[r], (w0[:, 0, 4 * P:], w0[:, 1, 4 * P:]))])
            yield EXP
            mark = SCAL.put(act_side, [mark, score_free[0]], lambda: A.activation(score0[:, :], ps[:, 0:ROWS * EXPERTS0], ACT.Exp, scale=-1.0))
            give(b, mark)
            yield
            score = DVE.put(dve_side, [mark], lambda: V.tensor_scalar(score0[:, :], score0[:, :], 1.0, None, ALU.add))
            half = ROWS * EXPERTS0 // 2
            for n in range(2):
                part = score0[:, n * half:(n + 1) * half]
                yield (1.45 if n else 0.3)
                score2 = DVE.put(dve_side, [score], lambda part=part: V.reciprocal(part, part))
            by_tok = [P, ROWS, EXPERTS0]
            row = lambda ap: ap.rearrange("p (r e) -> p r e", r=ROWS)
            choice = DVE.put(dve_side, [score2], lambda: V.tensor_tensor(
                row(sfc[:, :]), row(score0[:, :]), bias0[:, :].unsqueeze(1).to_broadcast(by_tok), ALU.add))
            yield 2
            grp = sfc[:, :].rearrange("p (g e) -> p g e", e=8)
            m = DVE.put(dve_side, [choice],
                        lambda: V.tensor_tensor(hi4[:, :, :], grp[:, :, 0:4], grp[:, :, 4:8], ALU.max),
                        lambda: V.tensor_tensor(lo4[:, :, :], grp[:, :, 0:4], grp[:, :, 4:8], ALU.min))
            yield 0.7
            m = DVE.put(dve_side, [m],
                        lambda: V.tensor_tensor(hi2[:, :, :], hi4[:, :, 0:2], hi4[:, :, 2:4], ALU.max),
                        lambda: V.tensor_tensor(mi2[:, :, :], hi4[:, :, 0:2], hi4[:, :, 2:4], ALU.min),
                        lambda: V.tensor_tensor(lo2[:, :, :], lo4[:, :, 0:2], lo4[:, :, 2:4], ALU.max))
            m = DVE.put(dve_side, [m], lambda: V.tensor_tensor(lo2[:, :, :], lo2[:, :, :], mi2[:, :, :], ALU.max))
            yield 0.9
            m = DVE.put(dve_side, [m],
                        lambda: V.tensor_tensor(mi2[:, :, 0], hi2[:, :, 0], hi2[:, :, 1], ALU.min),
                        lambda: V.tensor_tensor(g_a[:, :], hi2[:, :, 0], hi2[:, :, 1], ALU.max),
                        lambda: V.tensor_tensor(lo2[:, :, 0], lo2[:, :, 0], lo2[:, :, 1], ALU.max))
            m = DVE.chain(dve_side, [m],
                          lambda: V.tensor_tensor(lo2[:, :, 0], lo2[:, :, 0], mi2[:, :, 0], ALU.max),
                          lambda: V.tensor_tensor(g_a[:, :], g_a[:, :], lo2[:, :, 0], ALU.add))
            yield 0.9
            m = yield from rank_among_8(g_a[:, :].rearrange("p (r g) -> p r g", r=ROWS), ROWS,
                                        g_b[:, :].rearrange("p (r g) -> p r g", r=ROWS), [m, common_ready])
            yield 1.5
            m = DVE.chain(dve_side, [m],
                          lambda: V.tensor_scalar(g_b[:, :], g_b[:, :], TOP_GROUPS0 - 0.5, None, ALU.is_lt),
                          lambda: V.tensor_tensor(grp, grp, g_b[:, :].unsqueeze(2).to_broadcast([P, ROWS * GROUPS0, 8]), ALU.mult),
                          lambda: V.tensor_scalar(sfc[:, :], sfc[:, :], 0.0, None, ALU.add))
            yield 1.3
            m = DVE.put(dve_side, [m], *[lambda r=r: V.max(best0[:, r], row(sfc[:, :])[:, r]) for r in range(ROWS)])
            yield 0.9
            m = DVE.put(dve_side, [m], *[lambda r=r: V.match_replace(
                out=row(above)[:, r], in_to_replace=best0[:, r], in_values=row(sfc[:, :])[:, r], imm_value=FAR) for r in range(ROWS)])
            yield 0.9
            m = POOL.put(pool_side, [m], lambda: G.tensor_tensor(above, above, sfc[:, :], ALU.subtract))
            yield
            m = DVE.put(dve_side, [m], *[lambda r=r: V.scalar_tensor_tensor(
                row(above)[:, r], row(above)[:, r], 0.0, row(score0[:, :])[:, r], ALU.not_equal, ALU.mult,
                accum_out=wsum0[:, r:r + 1]) for r in range(ROWS)])
            score_free[0] = m
            yield 0.9
            m = DVE.chain(dve_side, [m],
                          lambda: V.tensor_scalar(wsum0[:, :], wsum0[:, :], EPS_W, None, ALU.add),
                          lambda: V.reciprocal(wsum0[:, :], wsum0[:, :]),
                          lambda: V.tensor_tensor(row(above), row(above), wsum0[:, :].unsqueeze(2).to_broadcast(by_tok), ALU.mult))
            yield 1
            m = POOL.put(pool_side, [m, coef_free[0]],
                        *[lambda n=n: G.tensor_scalar(coef[:, :, n], row(above), SCALE0, None, ALU.mult) for n in range(2)])
            yield
            yield
            yield from coef_to_columns(key, m)

        att1 = {"msg_free": [None] * 3}

        def setup1():
            over = [mark for _, mark, _ in free_banks] + [coefT_ready[CHUNKS - 1], mix_ready[CHUNKS - 1]]
            raw1 = scores[:, :, :].rearrange("p a b -> p (a b)")[:, 0:5 * P + EXPERTS1]
            raw_ready = SP.put(att1_raw_in, over, lambda: nc.sync.dma_start(raw1, att1_w), by=16)
            load(att1_in, causal[:, :], att1_c)
            load(att1_in, f1[:, :], att1_f)
            att1["in"] = load(att1_in, b1[:, :], att1_b)
            att1["zero"] = POOL.put(pool_setup, over + [coef_free[0]],
                                    lambda: G.memset(near[:, :, 0:WINDOW], 0.0),
                                    lambda: G.memset(coef[:, :, :, :], 0.0))
            yield
            yield
            parts = split_small(w1, raw1, [raw_ready, *over])
            yield
            b, ps, free = yield from take()
            mark = PE.put(pe_side, [parts, att1["in"], free],
                          *mm(ps[:, 0:P], w_m2T, w_ol), *mm(ps[:, P:2 * P], raw1[:, 2 * P:3 * P], w_og),
                          *mm(ps[:, 2 * P:2 * P + 1], w_ol, b_m2, stop=False), *mm(ps[:, 2 * P:2 * P + 1], w_og, b_v, start=False))
            hi = SCAL.put(act_side, [mark],
                          lambda: A.activation(w_local, ps[:, 0:P], ACT.Copy, scale=1.0 / WINDOW),
                          lambda: A.copy(w1[:, 0, 2 * P:3 * P], ps[:, P:2 * P]))
            yield
            att1["w"] = DVE.put(dve_side, [hi],
                                lambda: V.tensor_tensor(w1[:, 1, 2 * P:3 * P], ps[:, P:2 * P], f32(w1[:, 0, 2 * P:3 * P]), ALU.subtract),
                                lambda: V.tensor_tensor(b_o, ps[:, 2 * P:2 * P + 1], b_o, ALU.add))
            give(b, att1["w"])
            yield

        def w1_part(n):
            return (w1[:, 0, n * P:(n + 1) * P], w1[:, 1, n * P:(n + 1) * P])

        place = [(s, at, width) for s in range(SEQS) for at, width in KEYS]

        def attention1(key, c):
            xt, rows = columns_and_rows(key)
            b, ps, free = yield from take()
            mark = PE.put(pe_side, [xnT_ready[key], att1["w"], free], *mm3(ps[:, :], w1_part(0), xt))
            give(b, SCAL.put(act_side, [mark, att1["in"]], lambda ps=ps: A.activation(qT[:, :], ps[:, :], ACT.Identity, bias=b_q)))
            yield
            b, ps, free = yield from take()
            mark = PE.put(pe_side, [free], *mm3(ps[:, :], w1_part(1), xt))
            qk_ready = SCAL.put(act_side, [mark], lambda ps=ps: A.activation(kT[:, :], ps[:, :], ACT.Identity, bias=b_k))
            give(b, qk_ready)
            yield
            masked = []
            while c > 0 and key - 1 not in joined:
                yield
            for s in range(SEQS):
                b, ps, free = yield from take()
                mark = PE.put(pe_side, [qk_ready, free],
                              *[f for n, (at, width) in enumerate(KEYS) for f in
                                mm(ps[:, at:at + width], qT[:, s * SEQ + n * P:s * SEQ + (n + 1) * P], kT[:, s * SEQ:s * SEQ + width])])
                yield (0.8 if s else 0)
                m = DVE.put(dve_side, [mark, att1["in"], mix_free[0]],
                            lambda ps=ps, s=s: V.tensor_tensor(scores[:, s], ps[:, 0:KEYCOLS], causal[:, :], ALU.add))
                give(b, m)
                masked.append(m)
            yield 0.8
            side.add(f"messages {key}", local_messages(key, xt))
            m = DVE.put(dve_side, masked,
                        *[lambda r=r, s=s, at=at, wd=wd: V.max(best1[:, r], scores[:, s, at:at + wd]) for r, (s, at, wd) in enumerate(place)])
            yield 1.8
            scale = float(P) ** -0.5
            neg = DVE.put(dve_side, [m], lambda: V.tensor_scalar(top_neg[:, :], best1[:, :, 0], -scale, None, ALU.mult))
            for s in range(SEQS):
                m = DVE.put(dve_side, [m],
                            *[lambda r=r, s=s, at=at, wd=wd: V.match_replace(
                                out=rest[:, s, at:at + wd], in_to_replace=best1[:, r], in_values=scores[:, s, at:at + wd], imm_value=FAR)
                              for r, (q, at, wd) in enumerate(place) if q == s])
                chosen = POOL.put(pool_side, [m], lambda s=s: G.tensor_tensor(rest[:, s], rest[:, s], scores[:, s], ALU.subtract))
                yield (EXP if s else 1)
            e_mark = SCAL.put(act_side, [chosen, neg],
                              *[lambda r=r, s=s, at=at, wd=wd: A.activation(
                                  scores[:, s, at:at + wd], scores[:, s, at:at + wd], ACT.Exp, bias=top_neg[:, r:r + 1], scale=scale)
                                for r, (s, at, wd) in enumerate(place)])
            yield
            b, ps, free = yield from take()
            mark = PE.put(pe_side, [free], *[f for r in range(ROWS) for f in mm3(ps[:, r * P:(r + 1) * P], rows[r], w1_part(2))])
            v_ready = SCAL.put(act_side, [mark, mix_free[0]], lambda ps=ps: A.copy(v1[:, :], ps[:, :]))
            give(b, v_ready)
            yield
            for s in range(SEQS):
                p_sum = DVE.put(dve_side, [e_mark], *[lambda r=r, s=s, at=at, wd=wd: V.scalar_tensor_tensor(
                    rest[:, s, at:at + wd], rest[:, s, at:at + wd], 0.0, scores[:, s, at:at + wd], ALU.not_equal, ALU.mult,
                    accum_out=psum1[:, r:r + 1]) for r, (q, at, wd) in enumerate(place) if q == s])
                yield 1
            m = DVE.put(dve_side, [p_sum], lambda: V.reciprocal(psum1[:, :], psum1[:, :]))
            for s in range(SEQS):
                m2 = DVE.put(dve_side, [m],
                             *[lambda r=r, s=s, at=at, wd=wd: V.tensor_scalar(
                                 rest[:, s, at:at + wd], rest[:, s, at:at + wd], psum1[:, r:r + 1], None, ALU.mult)
                               for r, (q, at, wd) in enumerate(place) if q == s])
                yield 0.8
                b, ps, free = yield from take()
                mark = PE.put(pe_side, [m2, free],
                              *[lambda k=k, s=s, ps=ps: T.transpose(ps[:, k * P:(k + 1) * P], rest[:, s, k * P:(k + 1) * P], ident) for k in range(3)])
                pt = SCAL.put(act_side, [mark], lambda ps=ps, s=s: A.copy(scores[:, s], ps[:, 0:KEYCOLS]))
                give(b, pt)
            values_ready[key] = [pt, v_ready]

        def local_messages(key, xt):
            b, ps, free = yield from take()
            mark = PE.put(pe_side, [free], *mm3(ps[:, :], w1_part(4), xt))
            near_in = SCAL.put(act_side, [mark, att1["zero"]], lambda ps=ps: A.copy(near[:, :, WINDOW:], seqs(ps[:, :])))
            give(b, near_in)
            yield
            b_self, ps_self, free = yield from take()
            self_half = PE.put(pe_side, [free], *mm3(ps_self[:, :], w1_part(3), xt))
            yield
            heard = None
            msg_free = att1["msg_free"]
            for k in range(1, WINDOW + 1):
                slot = 0 if k == 1 else 1 + k % 2
                added = DVE.put(dve_side, [self_half, near_in, msg_free[slot]],
                                lambda k=k, slot=slot: V.tensor_tensor(
                                    seqs(msg[:, slot]), seqs(ps_self[:, :]), near[:, :, WINDOW - k:WINDOW - k + SEQ], ALU.add))
                if k == WINDOW:
                    give(b_self, added)
                yield 1
                act = SCAL.put(act_side, [added], lambda slot=slot: A.activation(msg[:, slot], msg[:, slot], ACT.Silu, bias=b_m1))
                if k > 1:
                    heard = POOL.put(pool_side, [act, heard, first_act], lambda slot=slot: G.tensor_tensor(msg[:, 0], msg[:, 0], msg[:, slot], ALU.add))
                    msg_free[slot] = heard
                else:
                    first_act = act
            mix_ready[key] = heard
            yield

        def routing1(key, c):
            yield from layer_norm(key, c, x1_ready[c])
            if c == 0:
                while CHUNKS - 1 not in mix_ready:
                    yield
                yield from setup1()
            _, rows = columns_and_rows(key)
            by_e = [P, ROWS, EXPERTS1]
            b, ps, free = yield from take()
            mark = PE.put(pe_side, [xnT_ready[key], att1["w"], free],
                          *[f for r in range(ROWS) for f in
                            router_products(ps, r, EXPERTS1, rows[r], w1[:, :, 5 * P:])])
            yield
            logits = ps[:, 0:ROWS * 2 * EXPERTS1].rearrange("p (r n e) -> p r n e", r=ROWS, n=2)
            m = DVE.chain(dve_side, [mark, att1["zero"]],
                          lambda: V.tensor_copy(gate[:, :, :], logits[:, :, 0]),
                          lambda: V.tensor_tensor(gate[:, :, :], logits[:, :, 1], gate[:, :, :], ALU.add),
                          lambda: V.tensor_reduce(gsum[:, :], gate[:, :, :], axis=AX, op=ALU.max),
                          lambda: V.tensor_tensor(gate[:, :, :], gate[:, :, :], gsum[:, :].unsqueeze(2).to_broadcast(by_e), ALU.subtract))
            give(b, m)
            yield EXP
            m = SCAL.put(act_side, [m], lambda: A.activation(gate[:, :, :], gate[:, :, :], ACT.Exp))
            yield
            m = DVE.chain(dve_side, [m],
                          lambda: V.tensor_reduce(gsum[:, :], gate[:, :, :], axis=AX, op=ALU.add),
                          lambda: V.reciprocal(gsum[:, :], gsum[:, :]),
                          lambda: V.tensor_tensor(gate[:, :, :], gate[:, :, :], gsum[:, :].unsqueeze(2).to_broadcast(by_e), ALU.mult))
            yield 0.7
            m = yield from rank_among_8(gate[:, :, :], ROWS, gsel[:, :, :], [m, common_ready])
            yield 1.2
            m = DVE.chain(dve_side, [m],
                          lambda: V.tensor_scalar(gsel[:, :, :], gsel[:, :, :], TOP1 - 0.5, None, ALU.is_lt),
                          lambda: V.tensor_tensor(gate[:, :, :], gate[:, :, :], gsel[:, :, :], ALU.mult),
                          lambda: V.tensor_reduce(gsum[:, :], gate[:, :, :], axis=AX, op=ALU.add))
            yield 0.7
            m = DVE.chain(dve_side, [m],
                          lambda: V.reciprocal(gsum[:, :], gsum[:, :]),
                          lambda: V.tensor_tensor(gate[:, :, :], gate[:, :, :], gsum[:, :].unsqueeze(2).to_broadcast(by_e), ALU.mult))
            twice = [P, ROWS, EXPERTS1, 2]
            m = DVE.put(dve_side, [m, coef_free[0]],
                        *[lambda n=n: V.tensor_copy(coef[:, :, n, 0:2 * EXPERTS1].rearrange("p r (e t) -> p r e t", t=2),
                                                    gate[:, :, :].unsqueeze(3).to_broadcast(twice)) for n in range(2)])
            yield 0.8
            yield from coef_to_columns(key, m)

        x1_ready = [None] * CHUNKS

        def finish(layer, c, y_mark):
            b, ps, free = yield from take()
            mark = PE.put(pe_side, [y_mark, free, common_ready],
                          *[lambda r=r: T.transpose(ps[:, r * P:(r + 1) * P], yT[:, r * P:(r + 1) * P], ident) for r in range(ROWS)])
            yT_free[0] = mark
            yield
            mark = DVE.put(dve_side, [mark], lambda: V.tensor_tensor(
                xres[:, c], ps[:, :].rearrange("p (r d) -> p r d", r=ROWS), xres[:, c], ALU.add))
            give(b, mark)
            x1_ready[c] = mark
            if layer == 1:
                SP.put(stored, [mark], lambda: nc.sync.dma_start(out_rows[c], xres[:, c]), by=16)
            yield 1

        tiles = [(0, c, j) for c in range(CHUNKS) for j in range(TILES0)] + \
                [(1, c, j) for c in range(CHUNKS) for j in range(TILES1)]
        hist = []

        picked = {}

        def routed_pair(g):
            layer, c, j = tiles[g]
            if layer == 0:
                return j if j < TILES0 - 1 else None
            return j // 2 if j % 2 == 0 else None

        def pick_experts(g):
            pair = routed_pair(g)
            if pair is None:
                return
            picked[g] = POOL.put(pool_pick, [common_ready, pick_free[pair % 2]], lambda: G.tensor_copy(
                pick_pair[:, pair % 2], pick[:, 2 * pair:2 * pair + 2].unsqueeze(2).to_broadcast([P, 2, 64])))

        def first_products(g):
            layer, c, j = tiles[g]
            key = c + layer * CHUNKS
            buf = key % 2
            xt = (xnT[:, buf, 0], xnT[:, buf, 1])
            w_gate, w_up, _ = tile_weights(j)
            m = {}
            two = hist[g - 2] if g >= 2 else {}
            split = list(w_split[j + layer * TILES0]) if c == 0 else []
            m["gate"] = PE.put(pe_gate, [xnT_ready[key], two.get("silu"), *split], *mm3(ps_gate[g % 2][:, :], w_gate, xt))
            if g >= 1:
                broadcast_coef(g - 1)
            m["up"] = PE.put(pe_up, [two.get("h1")], *mm3(ps_up[g % 2][:, :], w_up, xt))
            xnT_free[buf] = m["up"]
            hist.append(m)

        def broadcast_coef(g):
            layer, c, j = tiles[g]
            key = c + layer * CHUNKS
            m = hist[g]
            pair = routed_pair(g)
            if pair is not None:
                sel = pick_pair[:, pair % 2].rearrange("p a b -> p (a b)")
                m["coef"] = PE.put(pe_coef, [coefT_ready[key], picked[g], coef_read[0]],
                                   *mm(ps_coef[:, :], sel, coefT[:, key % 2]))
                coefT_free[key % 2] = pick_free[pair % 2] = m["coef"]
            else:
                m["coef"] = hist[g - 1]["coef"] if layer else None

        coef_read = [None]
        pick_free = [None, None]

        def times_coef(g):
            m = hist[g]
            s = g % 3
            if m["coef"] is None:
                m["h"] = m["h1"]
                return
            m["h"] = DVE.put(dve_coef, [m["h1"], m["coef"]],
                             lambda: V.tensor_tensor(silu_h[:, s], ps_coef[:, :], silu_h[:, s], ALU.mult))
            coef_read[0] = m["h"]

        def silu_and_up(g):
            m = hist[g]
            s = g % 3
            lo3 = hist[g - 3]["lo"] if g >= 3 else w0_ready
            m["silu"] = SCAL.put(act_silu, [m["gate"], lo3], lambda: A.activation(silu_h[:, s], ps_gate[g % 2][:, :], ACT.Silu))
            m["h1"] = DVE.put(dve_up, [m["silu"], m["up"]],
                              lambda: V.tensor_tensor(silu_h[:, s], ps_up[g % 2][:, :], silu_h[:, s], ALU.mult))

        def split_h(g):
            m = hist[g]
            s = g % 3
            down3 = hist[g - 3].get("down") if g >= 3 else None
            m["hi"] = SCAL.put(act_hi, [m["h"], down3], lambda: A.copy(h_hi[:, s], silu_h[:, s]))
            m["lo"] = POOL.put(pool_lo, [m["hi"], down3], lambda: G.tensor_tensor(h_lo[:, s], silu_h[:, s], f32(h_hi[:, s]), ALU.subtract))

        y_free = [None]

        def last_products(g):
            layer, c, j = tiles[g]
            m = hist[g]
            slot = g % 3
            key = c + layer * CHUNKS
            _, _, w_down = tile_weights(j)
            last = j == (TILES1 if layer else TILES0) - 1
            if last:
                if layer == 0:
                    products = mm(ps_y[:, :], w_out[:, :], mix_a[:, :], start=False, stop=False)
                else:
                    products = mm(ps_y[:, :], w_local, msg[:, 0], start=False, stop=False)
                    for s in range(SEQS):
                        v_a, v_b = (v1[:, r * P:(r + 1) * P] for r in (2 * s, 2 * s + 1))
                        at = s * SEQ
                        for dst, v, k in ((at, v_a, 0), (at + P, v_a, 1), (at + P, v_b, 2)):
                            products += mm(ps_y[:, dst:dst + P], v, scores[:, s, k * P:(k + 1) * P], start=False, stop=False)
                mix_free[0] = PE.put(pe_mix, [mix_ready[key], *values_ready.get(key, []), y_free[0], att0_ready if layer == 0 else att1["w"]], *products)
                joined.add(key)
                if layer:
                    att1["msg_free"][0] = mix_free[0]
            m["down"] = PE.put(pe_down, [m["hi"], m["lo"], y_free[0]],
                               *mm3(ps_y[:, :], w_down, (h_hi[:, slot], h_lo[:, slot]), start=j == 0, stop=last))
            if last:
                bias = b_o if layer else None
                copy = (lambda: A.activation(yT[:, :], ps_y[:, :], ACT.Identity, bias=bias)) if layer else \
                    (lambda: A.copy(yT[:, :], ps_y[:, :]))
                y_free[0] = SCAL.put(act_y, [m["down"], yT_free[0]], copy)
                yT_free[0] = y_free[0]
                return finish(layer, c, y_free[0])
            return None

        def drain(steps):
            for _ in steps:
                turn[0] += 1

        ROOM = [1.8, 3.5]
        PATIENCE = 3

        class Side:

            def __init__(self):
                self.pieces, self.held, self.patience, self.wait, self.room = [], [], 0, PATIENCE, 0.0

            def add(self, name, steps):
                self.pieces.append((name, steps))

            def step(self, piece):
                if piece in self.held:
                    self.patience -= 1
                    with_exp = sum(p[0].startswith(("attention", "route")) for p in self.pieces)
                    going = self.held if self.patience <= 0 or len(self.held) == with_exp else []
                else:
                    going = [piece]
                for one in going:
                    took = next(one[1], "end")
                    if one in self.held:
                        self.held = [p for p in self.held if p is not one]
                    if took == "end":
                        self.pieces = [p for p in self.pieces if p is not one]
                    elif took == EXP:
                        self.held = self.held + [one]
                        self.patience = self.wait
                    else:
                        self.room -= took or 0.0

            def turn(self, room):
                turn[0] += 1
                self.room = min(self.room + room, room)
                for piece in list(self.pieces):
                    if self.room > 0 and piece in self.pieces:
                        self.pieces = [p for p in self.pieces if p is not piece] + [piece]
                        self.step(piece)

            def finish(self, *names):
                while any(p[0] in names for p in self.pieces):
                    turn[0] += 1
                    for piece in list(self.pieces):
                        if piece in self.pieces:
                            self.step(piece)

        side = Side()
        splits = iter(range(TILES0))
        first_routing = routing0(0, 0)
        next(first_routing)
        w0_ready = split_small(w0, raw0, [att0_ready])
        side.add("route", first_routing)
        while any(name == "route" for name, _ in side.pieces):
            side.turn(ROOM[0])
            split_tile(0, next(splits))
        pick_experts(0)
        for g, (layer, c, j) in enumerate(tiles):
            done = None
            n_tiles = TILES1 if layer else TILES0
            if j == 0:
                side.wait = 0 if (layer, c) == (0, CHUNKS - 1) else PATIENCE
                side.add(f"attention {c + layer * CHUNKS}", attention1(CHUNKS + c, c) if layer else attention0(c, c))
            if j == LAG - 1 and g >= LAG:
                before = tiles[g - LAG][1] + tiles[g - LAG][0] * CHUNKS
                side.finish(f"attention {before}", f"messages {before}")
            first_products(g)
            if g >= LAG:
                done = last_products(g - LAG)
            if g >= 1:
                times_coef(g - 1)
            silu_and_up(g)
            if g + 1 < len(tiles):
                pick_experts(g + 1)
            if g >= 1:
                split_h(g - 1)
            for n in splits:
                split_tile(0, n)
                break
            if layer == 0 and c == CHUNKS - 1:
                k = j - LAG - 1
                if 0 <= k < TILES1:
                    split_tile(1, k, free=[hist[g - LAG - 1]["down"]])
            if layer == 0 and c == 0 and j == TILES0 - 1:
                for cc in range(3, CHUNKS):
                    x_ready[cc] = load(x_in[cc], xres[:, cc], x_rows[cc])
            if done is not None:
                side.add("finish", done)
            if j == 0:
                def route(layer=layer, c=c):
                    if layer == 0 and c < CHUNKS - 1:
                        yield from routing0(c + 1, c + 1)
                    elif layer == 0:
                        yield from routing1(CHUNKS, 0)
                    elif c < CHUNKS - 1:
                        yield from routing1(CHUNKS + c + 1, c + 1)
                side.add("route", route())
            side.turn(ROOM[layer])
            if j == n_tiles - 1:
                side.finish("route")
        n = len(tiles)
        for k in range(3):
            if k == 0:
                broadcast_coef(n - 1)
                times_coef(n - 1)
                split_h(n - 1)
            done = last_products(n - LAG + k)
            if k == 1:
                side.finish(f"attention {2 * CHUNKS - 1}", f"messages {2 * CHUNKS - 1}")
        drain(done)
        SP_last = (stored, stored.n)

        block = ctx.enter_context(nc.Block())

        @block.sync
        def _(eng):
            SP.run(eng)
            eng.wait_ge(SP_last[0].sem, SP_last[1])

        @block.tensor
        def _(eng):
            PE.run(eng)

        @block.vector
        def _(eng):
            DVE.run(eng)

        @block.scalar
        def _(eng):
            SCAL.run(eng)

        @block.gpsimd
        def _(eng):
            POOL.run(eng)


def shape_constants():
    ident = np.eye(P, dtype=np.float32)
    pick = (np.arange(P)[:, None] % 64 == np.arange(64)[None, :]).astype(np.float32)
    earlier = np.broadcast_to((np.arange(8)[None, :] < np.arange(8)[:, None]).astype(np.float32).reshape(1, 64), (P, 64))
    common = np.concatenate([ident, pick, earlier], 1)
    head = np.arange(P) // HEAD
    same_head = (head[:, None] == head[None, :]).astype(np.float32)
    inv_freq = (np.float32(1.0) / np.float32(ROPE_BASE) ** (np.arange(0, HEAD, 2, dtype=np.float32) / np.float32(HEAD))).astype(np.float32)
    freqs = np.arange(SEQ, dtype=np.float32)[:, None] * inv_freq[None, :]
    angle = np.tile(np.concatenate([freqs, freqs], 1), (1, HEADS))
    cos, sin = np.cos(angle), np.sin(angle)
    sign = np.where(np.arange(P) % HEAD < HEAD // 2, -1.0, 1.0).astype(np.float32)
    sin = sin * sign[None, :]
    scale = np.float32(HEAD ** -0.5)
    by_row = lambda t: t.reshape(2, P, P).transpose(1, 0, 2).reshape(P, SEQ)
    att0 = np.concatenate([same_head, cos.T * scale, sin.T * scale, by_row(cos), by_row(sin)], 1)
    tri = np.where(np.arange(P)[None, :] > np.arange(P)[:, None], FAR, 0.0)
    att1 = np.concatenate([tri, np.zeros((P, P)), tri], 1)
    return tuple(np.ascontiguousarray(t.astype(np.float32)) for t in (common, att0, att1))


def kernel(**inputs):
    import concourse.bacc as bacc
    from concourse.bass_utils import run_bass_kernel_spmd

    a = {k: np.asarray(v) for k, v in inputs.items()}
    cat = np.concatenate
    common_c, att0_c, att1_c = shape_constants()

    pairs = EXPERTS0 * FF0 // P

    def paired(w):
        return w.reshape(pairs, 2, P, FF0).transpose(0, 2, 1, 3).reshape(pairs, P, P)

    tiles0 = cat([paired(a["L0_ffn_Wg"]), paired(a["L0_ffn_Wu"]), a["L0_ffn_Wd"].reshape(pairs, P, P)], 2)
    shared = cat([a["L0_ffn_SWg"], a["L0_ffn_SWu"], a["L0_ffn_SWd"]], 1)[None]

    def halves(w):
        return w.reshape(TILES1, P, P).transpose(0, 2, 1)

    down1 = a["L1_ffn_w2"].reshape(EXPERTS1, P, 2, P).transpose(0, 2, 3, 1).reshape(TILES1, P, P)
    tiles1 = cat([halves(a["L1_ffn_w1"]), halves(a["L1_ffn_w3"]), down1], 2)
    ffn_w = cat([tiles0, shared, tiles1], 0)
    wq, wk, wv = np.split(a["L0_attn_W_qkv"], 3, axis=1)
    swap = (np.arange(P) // HEAD) * HEAD + (np.arange(P) % HEAD + HEAD // 2) % HEAD
    att0_w = cat([wq, wq[:, swap], wk, wv, a["L0_ffn_router_w"].T], 1)
    wm1, wo = a["L1_attn_Wm1"], a["L1_attn_Wo"]
    att1_w = cat([a["L1_attn_Wq"], a["L1_attn_Wk"], a["L1_attn_Wv"].T, wm1[:P], wm1[P:], a["L1_ffn_gate_w"].T], 1)
    att1_f = cat([a["L1_attn_Wm2"].T, wo[:P], wo[P:]], 1)
    att1_b = np.stack([a[f"L1_attn_{n}"] for n in ("bq", "bk", "bv", "bm1", "bm2", "bo")], 1)
    arrays = {
        "x": a["L0_attn_x"].reshape(TOKENS, P), "ffn_w": ffn_w, "att0_w": att0_w, "att0_f": a["L0_attn_W_out"],
        "att0_c": att0_c, "e_bias": a["L0_ffn_e_bias"], "att1_w": att1_w, "att1_f": att1_f, "att1_b": att1_b,
        "att1_c": att1_c, "common_c": common_c,
    }
    arrays = {k: np.ascontiguousarray(v) for k, v in arrays.items()}
    nc = bacc.Bacc("TRN2", target_bir_lowering=False, num_devices=1)
    args = [nc.dram_tensor(f"in_{k}", v.shape, mybir.dt.from_np(v.dtype), kind="ExternalInput").ap() for k, v in arrays.items()]
    out = nc.dram_tensor("out", (TOKENS, P), FP32, kind="ExternalOutput").ap()
    build_program(nc, *args, out)
    r = run_bass_kernel_spmd(nc, [{f"in_{k}": v for k, v in arrays.items()}], core_ids=[0])
    return r.results[0]["out"].reshape(a["L0_attn_x"].shape)
```
